# Optimizing a Trainium2 kernel written in Bass

```python
import numpy as np
import jax
import jax.numpy as jnp

def _softmax(x, axis=-1):
    return jax.nn.softmax(x, axis=axis)
def _gelu(x):
    return jax.nn.gelu(x, approximate=True)
def _silu(x):
    return jax.nn.silu(x)
def _sigmoid(x):
    return jax.nn.sigmoid(x)
def _layernorm(x, axis=-1, eps=1e-5):
    m = jnp.mean(x, axis=axis, keepdims=True)
    v = jnp.var(x, axis=axis, keepdims=True)
    return (x - m) / jnp.sqrt(v + eps)
def _scatter_add(tgt, idx, src, axis=0):
    return tgt.at[idx].add(src)
def _segment_sum(src, seg, n):
    return jax.ops.segment_sum(src, seg, n)

kernel_name = 'mk_adj_preln_d4_adj_256_480bb4'

def setup_inputs(seed: int = 0):
    np.random.seed(seed)
    _w = jnp.asarray
    def _rec_inputs():
        import jax
        import jax.numpy as jnp
        _gk = jax.random.key(seed)
        x = -0.0002928 + 1 * jax.random.normal(jax.random.fold_in(_gk, 1), (32, 512, 256), jnp.float32)
        _a = jax.random.bernoulli(jax.random.fold_in(_gk, 2), 0.0078125, (32, 512, 512))
        _a = jnp.logical_or(_a, jnp.swapaxes(_a, -1, -2))
        _a = jnp.logical_or(_a, jnp.eye(512, dtype=bool))
        _af = _a.astype(jnp.float32)
        _af = _af * jax.random.uniform(jax.random.fold_in(_gk, 3), (32, 512, 512), jnp.float32, 0.05, 1)
        adj = _af
        _nm = jnp.ones((32, 512), dtype=bool)
        nodemask = jnp.where(_nm, 1.0, 0.0).astype(jnp.float32)
        return x, adj, nodemask
    x, adj, nodemask = _rec_inputs()
    def _L0_gnn_setup():
        import jax, jax.numpy as jnp
        import numpy as np
        B, N, D, H = (8, 2048, 256, 1024)
        RMS_EPS = 1e-06

        def _rmsnorm(h, w, eps=RMS_EPS):
            var = jnp.mean(jnp.square(h), axis=-1, keepdims=True)
            return h * jax.lax.rsqrt(var + eps) * w
        key = jax.random.key(seed)
        ks = jax.random.split(key, 5)
        x = jax.random.normal(ks[0], (B, N, D), dtype=jnp.float32)
        adjacency = jax.random.uniform(ks[1], (B, N, N), dtype=jnp.float32)
        epsilon = jnp.zeros((), dtype=jnp.float32)
        W1 = jax.random.normal(ks[2], (D, H), dtype=jnp.float32) * (1.0 / np.sqrt(D))
        b1 = jnp.zeros((H,), dtype=jnp.float32)
        rms_weight = jnp.ones((H,), dtype=jnp.float32)
        W2 = jax.random.normal(ks[3], (H, D), dtype=jnp.float32) * (1.0 / np.sqrt(H))
        b2 = jnp.zeros((D,), dtype=jnp.float32)
        return {'x': x, 'adjacency': adjacency, 'epsilon': epsilon, 'W1': W1, 'b1': b1, 'rms_weight': rms_weight, 'W2': W2, 'b2': b2}
    _L0_gnn_all = _L0_gnn_setup()
    _L0_gnn_in = {k: v for k, v in _L0_gnn_all.items() if k in ('epsilon', 'W1', 'b1', 'rms_weight', 'W2', 'b2', )}
    del _L0_gnn_all

    def _L1_gnn_setup():
        import jax, jax.numpy as jnp
        import numpy as np
        B, N, IN_DIM, OUT_DIM = (8, 2048, 256, 256)
        EDGE_P = 0.02
        MASK_P = 0.9
        key = jax.random.key(seed)
        ks = jax.random.split(key, 8)
        x = jax.random.normal(ks[0], (B, N, IN_DIM), dtype=jnp.float32)
        adj = (jax.random.uniform(ks[1], (B, N, N)) < EDGE_P).astype(jnp.float32)
        mask = (jax.random.uniform(ks[2], (B, N)) < MASK_P).astype(jnp.float32)
        lim1 = 1.0 / np.sqrt(IN_DIM)
        W = jax.random.uniform(ks[3], (OUT_DIM, IN_DIM), minval=-lim1, maxval=lim1, dtype=jnp.float32)
        b = jax.random.uniform(ks[4], (OUT_DIM,), minval=-lim1, maxval=lim1, dtype=jnp.float32)
        lim2 = 1.0 / np.sqrt(2 * OUT_DIM)
        a1 = jax.random.uniform(ks[5], (OUT_DIM,), minval=-lim2, maxval=lim2, dtype=jnp.float32)
        a2 = jax.random.uniform(ks[6], (OUT_DIM,), minval=-lim2, maxval=lim2, dtype=jnp.float32)
        att_b = jax.random.uniform(ks[7], (), minval=-lim2, maxval=lim2, dtype=jnp.float32)
        return {'x': x, 'adj': adj, 'mask': mask, 'W': W, 'b': b, 'a1': a1, 'a2': a2, 'att_b': att_b}
    _L1_gnn_all = _L1_gnn_setup()
    _L1_gnn_in = {k: v for k, v in _L1_gnn_all.items() if k in ('W', 'b', 'a1', 'a2', 'att_b', )}
    del _L1_gnn_all

    def _L2_gnn_setup():
        import math
        import jax, jax.numpy as jnp
        import numpy as np
        B, N, D, H = (32, 512, 256, 8)
        HD = D // H
        key = jax.random.key(seed)
        ks = jax.random.split(key, 9)
        h = jax.random.normal(ks[0], (B, N, D), dtype=jnp.float32)
        edge = jax.random.normal(ks[1], (B, N, N), dtype=jnp.float32)
        adj = jax.random.uniform(ks[2], (B, N, N)) < 0.5
        adj_mask = adj | jnp.eye(N, dtype=bool)[None]
        s = 1.0 / math.sqrt(D)
        W_q = jax.random.normal(ks[3], (D, D), dtype=jnp.float32) * s
        W_k = jax.random.normal(ks[4], (D, D), dtype=jnp.float32) * s
        W_v = jax.random.normal(ks[5], (D, D), dtype=jnp.float32) * s
        W_e = jax.random.normal(ks[6], (H, 1), dtype=jnp.float32)
        W_o = jax.random.normal(ks[7], (D, D), dtype=jnp.float32) * s
        return {'h': h, 'edge': edge, 'adj_mask': adj_mask, 'W_q': W_q, 'W_k': W_k, 'W_v': W_v, 'W_e': W_e, 'W_o': W_o}
    _L2_gnn_all = _L2_gnn_setup()
    _L2_gnn_in = {k: v for k, v in _L2_gnn_all.items() if k in ('W_q', 'W_k', 'W_v', 'W_e', 'W_o', )}
    del _L2_gnn_all

    def _L3_gnn_setup():
        import jax, jax.numpy as jnp
        import numpy as np
        B, N, C_IN, C_OUT = (8, 2048, 256, 256)
        key = jax.random.key(seed)
        k1, k2, k3 = jax.random.split(key, 3)
        x = jax.random.normal(k1, (B, N, C_IN), dtype=jnp.float32)
        adj = jax.random.uniform(k2, (B, N, N), dtype=jnp.float32)
        limit = float(np.sqrt(6.0 / (C_IN + C_OUT)))
        weight = jax.random.uniform(k3, (C_IN, C_OUT), minval=-limit, maxval=limit, dtype=jnp.float32)
        bias = jnp.zeros((C_OUT,), dtype=jnp.float32)
        return {'x': x, 'adj': adj, 'weight': weight, 'bias': bias}
    _L3_gnn_all = _L3_gnn_setup()
    _L3_gnn_in = {k: v for k, v in _L3_gnn_all.items() if k in ('weight', 'bias', )}
    del _L3_gnn_all

    return {
        "x": x,
        "adj": adj,
        "nodemask": nodemask,
        "L0_gnn_epsilon": _L0_gnn_in["epsilon"],
        "L0_gnn_W1": _L0_gnn_in["W1"],
        "L0_gnn_b1": _L0_gnn_in["b1"],
        "L0_gnn_rms_weight": _L0_gnn_in["rms_weight"],
        "L0_gnn_W2": _L0_gnn_in["W2"],
        "L0_gnn_b2": _L0_gnn_in["b2"],
        "L1_gnn_W": _L1_gnn_in["W"],
        "L1_gnn_b": _L1_gnn_in["b"],
        "L1_gnn_a1": _L1_gnn_in["a1"],
        "L1_gnn_a2": _L1_gnn_in["a2"],
        "L1_gnn_att_b": _L1_gnn_in["att_b"],
        "L2_gnn_W_q": _L2_gnn_in["W_q"],
        "L2_gnn_W_k": _L2_gnn_in["W_k"],
        "L2_gnn_W_v": _L2_gnn_in["W_v"],
        "L2_gnn_W_e": _L2_gnn_in["W_e"],
        "L2_gnn_W_o": _L2_gnn_in["W_o"],
        "L3_gnn_weight": _L3_gnn_in["weight"],
        "L3_gnn_bias": _L3_gnn_in["bias"],
    }

def reference(x, adj, nodemask, L0_gnn_epsilon, L0_gnn_W1, L0_gnn_b1, L0_gnn_rms_weight, L0_gnn_W2, L0_gnn_b2, L1_gnn_W, L1_gnn_b, L1_gnn_a1, L1_gnn_a2, L1_gnn_att_b, L2_gnn_W_q, L2_gnn_W_k, L2_gnn_W_v, L2_gnn_W_e, L2_gnn_W_o, L3_gnn_weight, L3_gnn_bias):
    import jax
    import jax.numpy as jnp
    def _L0_gnn_ref(x, adjacency, epsilon, W1, b1, rms_weight, W2, b2):
        import jax, jax.numpy as jnp
        import numpy as np
        B, N, D, H = (8, 2048, 256, 1024)
        RMS_EPS = 1e-06

        def _rmsnorm(h, w, eps=RMS_EPS):
            var = jnp.mean(jnp.square(h), axis=-1, keepdims=True)
            return h * jax.lax.rsqrt(var + eps) * w
        neighbor_sum = jnp.einsum('bnm,bmd->bnd', adjacency, x)
        agg = epsilon * x + neighbor_sum
        h = jnp.einsum('bnd,dh->bnh', agg, W1) + b1
        h = jax.nn.silu(_rmsnorm(h, rms_weight))
        out = jnp.einsum('bnh,hd->bnd', h, W2) + b2
        return out

    def _L1_gnn_ref(x, adj, mask, W, b, a1, a2, att_b):
        import jax, jax.numpy as jnp
        import numpy as np
        B, N, IN_DIM, OUT_DIM = (8, 2048, 256, 256)
        EDGE_P = 0.02
        MASK_P = 0.9
        h = jnp.einsum('bni,di->bnd', x, W) + b
        s1 = h @ a1
        s2 = h @ a2
        logits = s1[:, :, None] + s2[:, None, :] + att_b
        att = jax.nn.sigmoid(logits) * adj
        att = att * mask[:, :, None] * mask[:, None, :]
        att = att / (jnp.sum(att, axis=-1, keepdims=True) + 1e-08)
        h_new = jnp.einsum('bij,bjd->bid', att, h)
        return h_new * mask[:, :, None]

    def _L2_gnn_ref(h, edge, adj_mask, W_q, W_k, W_v, W_e, W_o):
        import math
        import jax, jax.numpy as jnp
        import numpy as np
        B, N, D, H = (32, 512, 256, 8)
        HD = D // H
        b, n, _ = h.shape
        q = (h @ W_q.T).reshape(b, n, H, HD).transpose(0, 2, 1, 3)
        k = (h @ W_k.T).reshape(b, n, H, HD).transpose(0, 2, 1, 3)
        v = (h @ W_v.T).reshape(b, n, H, HD).transpose(0, 2, 1, 3)
        edge_bias = jnp.einsum('bij,h->bhij', edge, W_e[:, 0])
        scores = jnp.einsum('bhid,bhjd->bhij', q, k) / math.sqrt(HD) + edge_bias
        scores = jnp.where(adj_mask[:, None], scores, -jnp.inf)
        attn = jax.nn.softmax(scores, axis=-1)
        out = jnp.einsum('bhij,bhjd->bhid', attn, v)
        out = out.transpose(0, 2, 1, 3).reshape(b, n, D)
        return out @ W_o.T

    def _L3_gnn_ref(x, adj, weight, bias):
        import jax, jax.numpy as jnp
        import numpy as np
        B, N, C_IN, C_OUT = (8, 2048, 256, 256)
        d_inv_sqrt = (jnp.sum(adj, axis=-1) + 1e-05) ** (-0.5)
        adj_norm = d_inv_sqrt[..., :, None] * adj * d_inv_sqrt[..., None, :]
        support = jnp.einsum('bni,io->bno', x, weight)
        return jnp.einsum('bnm,bmo->bno', adj_norm, support) + bias

    h = jnp.maximum(_layernorm(x, axis=-1), 0.0)
    x = x + _L0_gnn_ref(h, adj, L0_gnn_epsilon, L0_gnn_W1, L0_gnn_b1, L0_gnn_rms_weight, L0_gnn_W2, L0_gnn_b2)
    h = jnp.maximum(_layernorm(x, axis=-1), 0.0)
    x = x + _L1_gnn_ref(h, adj, nodemask, L1_gnn_W, L1_gnn_b, L1_gnn_a1, L1_gnn_a2, L1_gnn_att_b)
    h = jnp.maximum(_layernorm(x, axis=-1), 0.0)
    x = x + _L2_gnn_ref(h, adj, adj, L2_gnn_W_q, L2_gnn_W_k, L2_gnn_W_v, L2_gnn_W_e, L2_gnn_W_o)
    h = jnp.maximum(_layernorm(x, axis=-1), 0.0)
    x = x + _L3_gnn_ref(h, adj, L3_gnn_weight, L3_gnn_bias)
    return x


_drawn_inputs = setup_inputs


def setup_inputs(seed=0):
    import zlib

    import numpy as np

    out = dict(_drawn_inputs(seed))
    spreads = {'L0_gnn_b1': (0.0, 0.1),
     'L0_gnn_rms_weight': (1.0, 0.2),
     'L0_gnn_b2': (0.0, 0.1),
     'L3_gnn_bias': (0.0, 0.1)}
    factors = {'L1_gnn_a1': 24.414, 'L1_gnn_a2': 8.0}
    for name, (base, spread) in spreads.items():
        noise = np.random.default_rng([zlib.crc32(name.encode()), seed]).standard_normal(out[name].shape)
        drawn = base * np.exp(spread * noise) if base else spread * noise
        out[name] = jnp.asarray(drawn.astype(out[name].dtype))
    for name, factor in factors.items():
        out[name] = (out[name] * factor).astype(out[name].dtype)
    return out
```

```python
from contextlib import ExitStack

import concourse.bass as bass
from concourse import mybir

ALU = mybir.AluOpType
ACT = mybir.ActivationFunctionType
AX = mybir.AxisListType
F32 = mybir.dt.float32
F32R = mybir.dt.float32r
BF16 = mybir.dt.bfloat16

P = 128
BIG = 1e37
TINY = 1e-20
LN_EPS, RMS_EPS, ATT_EPS, DEG_EPS = 1e-5, 1e-6, 1e-8, 1e-5


def at(t, per_batch, k):
    return t * per_batch + k


def gnn_kernel(nc, x, adj, adjT, maskT, W1, b1, rmsw, W2, b2, WL, WLn, bL, WqT, WkT, WvT, WoT, W3, b3, cols, out):
    B, N, D = x.shape
    H = 8
    HD = D // H
    F = W1.shape[1]
    NT, DT, FT = N // P, D // P, F // P
    HG = P // HD
    SC = HD ** -0.5
    DE = D + 2

    with ExitStack() as ctx:
        def sb(name, shape, dt=F32):
            return ctx.enter_context(nc.sbuf_tensor(name, shape, dt))

        def sem(name):
            return ctx.enter_context(nc.semaphore(name))

        w1_hi, w1_lo = (sb(f"w1_{s}", [P, DT, F], F32R) for s in ("hi", "lo"))
        w2_hi, w2_lo = (sb(f"w2_{s}", [P, FT, D], F32R) for s in ("hi", "lo"))
        ws_hi, ws_lo = (sb(f"ws_{s}", [P, 5, DT, D], F32R) for s in ("hi", "lo"))
        wl_hi, wl_lo = (sb(f"wl_{s}", [P, DT, DE], F32R) for s in ("hi", "lo"))
        wa_hi, wa_lo = (sb(f"wa_{s}", [P, DT, P], F32R) for s in ("hi", "lo"))
        WQ, WK, WV, WO, WG = range(5)
        b1_rows = sb("b1_rows", [P, F], F32R)
        ones_rows = sb("ones_rows", [P, P], F32R)
        rmsw_b = sb("rmsw_b", [P, F])
        bL_b, b2_b, b3_b = sb("bL_b", [P, D]), sb("b2_b", [P, D]), sb("b3_b", [P, D])
        ident = sb("ident", [P, P])
        neg_mask = sb("neg_mask", [P, H, P], BF16)
        cst = sb("cst", [P, 18])
        drv = sb("drv", [P, 64])
        neg_w = drv[:, 0:8]
        q_scale = drv[:, 8:10]
        s_const = drv[:, 10:11]
        k_rms, k_ln, k_mhalf, k_deg, k_neg1 = (drv[:, 11 + i:12 + i] for i in range(5))
        k_zero, one_b = drv[:, 40:41], drv[:, 41:45]
        t8, t8b = drv[:, 16:24], drv[:, 24:32]
        t2, t2b, t2c = drv[:, 32:34], drv[:, 34:36], drv[:, 36:38]

        x_in = sb("x_in", [P, NT, D])
        x_sb = sb("x_sb", [P, NT, D])
        adj_sb = sb("adj_sb", [P, NT, N])
        adjT_sb = sb("adjT_sb", [P, NT, N])
        o_f32 = adjT_sb[:, 0:DT, :]
        aT_hi, aT_lo = (sb(f"aT_{s}", [P, NT, N], F32R) for s in ("hi", "lo"))
        unlinked = sb("unlinked", [P, NT, N], BF16)
        v_hi, v_lo = (sb(f"v_{s}", [P, NT * DE], F32R) for s in ("hi", "lo"))
        rows_hi, rows_lo = (v[:, :].rearrange("p (n d) -> p n d", n=NT) for v in (v_hi, v_lo))
        qk_hi, qk_lo = (v[:, 0:2 * N].rearrange("p (s n) -> p s n", s=2) for v in (v_hi, v_lo))
        k_hi, k_lo = (sb(f"k_{s}", [P, DT, N], F32R) for s in ("hi", "lo"))
        T_hi, T_lo = (sb(f"T_{s}", [P, DT, N], F32R) for s in ("hi", "lo"))
        r16 = sb("r16", [P, 2, 2048], F32R)
        s_hi, s_lo = (r16[:, i, :].rearrange("p (b f n) -> p b f n", b=2, n=P) for i in range(2))
        att_hi, att_lo = (r16[:, i, :].rearrange("p (m n) -> p m n", m=NT) for i in range(2))
        q_stack, k_stack = (r16[:, i, :].rearrange("p (s n) -> p s n", s=4) for i in range(2))
        big = sb("big", [P, 8192])
        pT = big[:, :].rearrange("p (h j n) -> p h j n", h=HG, j=NT)
        hid = big[:, 0:2048].rearrange("p (b n) -> p b n", b=2)
        sig = big[:, 2048:3072].rearrange("p (b n) -> p b n", b=2)
        att = big[:, 3072:4096].rearrange("p (b n) -> p b n", b=2)
        h_f32 = big[:, 4096:5120].rearrange("p (n d) -> p n d", n=NT)
        junk = big[:, 5120:6144].rearrange("p (b n) -> p b n", b=2)
        msg = big[:, 6144:7168].rearrange("p (n d) -> p n d", n=NT)
        diag = big[:, 7168:7680].rearrange("p (n d) -> p n d", n=NT)
        vals = sb("vals", [P, NT, D])
        prob = sb("prob", [P, 6, N])
        mask_sb = sb("mask_sb", [P, NT])
        small = sb("small", [P, 256])
        bn = small[:, 0:24].rearrange("p (n k) -> p n k", n=NT)
        mv = small[:, 24:32].rearrange("p (n k) -> p n k", n=NT)
        ve, rstd, nmean, nb = (small[:, 32 + 4 * i:36 + 4 * i] for i in range(4))
        ss = small[:, 48:56].rearrange("p (n c) -> p n c", n=NT)
        sse, rms = small[:, 56:60], small[:, 60:64]
        s2 = small[:, 64:68]
        den, rec, fac = small[:, 68:72], small[:, 72:76], small[:, 76:80]
        deg, dege, dinv = small[:, 80:84], small[:, 84:88], small[:, 88:92]
        nmax = small[:, 96:128].rearrange("p (h n) -> p h n", h=H)
        psum_ = small[:, 128:160].rearrange("p (h n) -> p h n", h=H)
        pinv = small[:, 160:192].rearrange("p (h n) -> p h n", h=H)
        fence = small[:, 200:201]
        inv_x = sb("inv_x", [P, NT, HG, HD])

        tp = [ctx.enter_context(nc.psum_tensor(f"tp{i}", [P, N], F32)) for i in range(2)]
        mm = [ctx.enter_context(nc.psum_tensor(f"mm{i}", [P, N], F32)) for i in range(6)]

        x_loaded, adj_loaded, adjT_loaded, mask_loaded, out_stored = (
            sem(n) for n in ("x_loaded", "adj_loaded", "adjT_loaded", "mask_loaded", "out_stored"))
        stacked = [sem(f"stacked{i}") for i in range(4)]
        waited = sem("waited")
        w_loaded, setup_dve, setup_act, setup_pool, setup_pe = (
            sem(n) for n in ("w_loaded", "setup_dve", "setup_act", "setup_pool", "setup_pe"))
        stats, N_stats = sem("stats"), 16
        means, N_means = sem("means"), 16
        fenced, N_fenced = sem("fenced"), 4
        normed, N_normed = sem("normed"), 4
        pool_step, N_pool = sem("pool_step"), 3 * 4 + 4 + 1
        h_ready, N_h = sem("h_ready"), 16
        h_hi_ready, h_lo_ready = sem("h_hi_ready"), sem("h_lo_ready")
        aT_hi_ready, aT_lo_ready, N_aT = sem("aT_hi_ready"), sem("aT_lo_ready"), 3
        diag_ready = sem("diag_ready")
        xb2_ready, xb3_ready = sem("xb2_ready"), sem("xb3_ready")
        agg_ps = sem("agg_ps")
        T_hi_ready, T_lo_ready, N_T = sem("T_hi_ready"), sem("T_lo_ready"), 10
        hid_ps = sem("hid_ps")
        squared = sem("squared")
        rms_ready = sem("rms_ready")
        rms_eps = sem("rms_eps")
        hid_ready = sem("hid_ready")
        silu_done = sem("silu_done")
        tp_full, N_tp = sem("tp_full"), 8 + 2 + 2 + 32 + 2 + 2
        s_hi_ready, s_lo_ready = sem("s_hi_ready"), sem("s_lo_ready")
        y_ps, N_y = sem("y_ps"), 16
        x_ready, N_x = sem("x_ready"), 16
        lin_ps = sem("lin_ps")
        s1_ps = sem("s1_ps")
        lin_hi_ready, lin_lo_ready = sem("lin_hi_ready"), sem("lin_lo_ready")
        s2_ready = sem("s2_ready")
        sig_ready, att_ready, att_hi_ready, att_lo_ready = (
            sem(n) for n in ("sig_ready", "att_ready", "att_hi_ready", "att_lo_ready"))
        ones_ready, rowsum_ready = sem("ones_ready"), sem("rowsum_ready")
        upd_step = sem("upd_step")
        qk_ps, v_ps = sem("qk_ps"), sem("v_ps")
        qk_hi_ready, qk_lo_ready, v_ready = sem("qk_hi_ready"), sem("qk_lo_ready"), sem("v_ready")
        sc_ps = sem("sc_ps")
        biased = sem("biased")
        exped = sem("exped")
        pT_act, pT_dve = sem("pT_act"), sem("pT_dve")
        av_ps = sem("av_ps")
        inv_ready, invx_ready = sem("inv_ready"), sem("invx_ready")
        lb_ready, o_ready = sem("lb_ready"), sem("o_ready")
        deg_ready, dinv_ready, unlinked_ready = sem("deg_ready"), sem("dinv_ready"), sem("unlinked_ready")
        sup_ps = sem("sup_ps")
        sup_hi_ready, sup_lo_ready = sem("sup_hi_ready"), sem("sup_lo_ready")

        SETUP_DVE = 43

        def diag_of(tile):
            return bass.AP(tensor=tile, offset=0, ap=[[NT * N, P], [N + P, NT], [1, P]])

        def later(t):
            return not isinstance(t, int) or t > 0

        freed = []
        for i in range(8):
            freed.append([(s_hi_ready, 8, i + 1), (s_lo_ready, 8, i + 1)])
        for i in (3, 4, 5, 6):
            freed.append([(T_hi_ready, N_T, i), (T_lo_ready, N_T, i)])
        n_act = n_dve = 0
        tp_of_prob, tp_of_inv = {}, {}
        for h in range(H):
            for j in range(NT):
                tp_of_prob[h, j] = len(freed)
                if j < 3:
                    n_act += 1
                    freed.append([(pT_act, 24, n_act)])
                else:
                    n_dve += 1
                    freed.append([(pT_dve, 8, n_dve)])
            if h in (HG, H - 1):
                g = 0 if h == HG else 1
                tp_of_inv[g] = len(freed)
                freed.append([(lb_ready, 2, g + 1)])
        tp_of_L3 = len(freed)
        for i in (9, 10):
            freed.append([(T_hi_ready, N_T, i), (T_lo_ready, N_T, i)])
        assert len(freed) == N_tp and N_tp % 2 == 0

        def wait_tp_free(pe, t, k):
            if k >= 2:
                for s, per, n in freed[k - 2]:
                    pe.wait_ge(s, at(t, per, n))
            else:
                for s, per, n in freed[N_tp - 2 + k]:
                    if later(t):
                        pe.wait_ge(s, t * per)

        def unregistered(eng):
            eng.sem_inc(waited)

        block = ctx.enter_context(nc.Block())

        @block.sync
        def _(sp):
            stage = big
            kp = "(k p) n -> p k n"
            sp.dma_start(stage[:, 0:2048].rearrange("p (k n) -> p k n", k=DT), W1.rearrange(kp, p=P)).then_inc(w_loaded, 16)
            sp.dma_start(stage[:, 2048:4096].rearrange("p (k n) -> p k n", k=FT), W2.rearrange(kp, p=P)).then_inc(w_loaded, 16)
            for i, w in enumerate((WqT, WkT, WvT, WoT, W3, WL, WLn)):
                o = 4096 + 512 * i
                sp.dma_start(stage[:, o:o + 512].rearrange("p (k n) -> p k n", k=DT), w.rearrange(kp, p=P)).then_inc(w_loaded, 16)
            b1_stage = prob[:, 0:2, :].rearrange("p a n -> p (a n)")
            for r in (0, 32):
                sp.dma_start(b1_stage[r:r + 1, :], b1[None, :]).then_inc(w_loaded, 16)
            sp.dma_start(rmsw_b[:, :], rmsw[None, :].to_broadcast([P, F])).then_inc(w_loaded, 16)
            for d, s in ((bL_b, bL), (b2_b, b2), (b3_b, b3)):
                sp.dma_start(d[:, :], s[None, :].to_broadcast([P, D])).then_inc(w_loaded, 16)
            sp.dma_start(cst[:, :], cols).then_inc(w_loaded, 16)

            rows = "o (n p) d -> p (o n) d"

            def load_x(b):
                sp.dma_start(x_in[:, :, :], x[bass.ds(b, 1)].rearrange(rows, p=P)).then_inc(x_loaded, 16)

            def load_mask(b):
                sp.dma_start(mask_sb[:, :], maskT[bass.ds(b, 1)].rearrange("o p n -> p (o n)")).then_inc(mask_loaded, 16)

            def load_adj(b):
                sp.dma_start(adj_sb[:, :, :], adj[bass.ds(b, 1)].rearrange(rows, p=P)).then_inc(adj_loaded, 16)

            def load_adjT(b):
                sp.dma_start(adjT_sb[:, :, :], adjT[bass.ds(b, 1)].rearrange(rows, p=P)).then_inc(adjT_loaded, 16)

            def batch(t, last):
                def stack(h):
                    g, s, r = h // HG, h % 4, slice(HD * (h % HG), HD * (h % HG) + HD)
                    if h < 4:
                        sp.wait_ge(y_ps, at(t, N_y, 8))
                        unregistered(sp)
                    else:
                        sp.wait_ge(sc_ps, at(t, 32, 4 * (h - 4) + 4))
                        unregistered(sp)
                    sp.wait_ge(qk_hi_ready, at(t, 4, 2 * g + 2))
                    unregistered(sp)
                    sp.wait_ge(qk_lo_ready, at(t, 4, 2 * g + 2))
                    unregistered(sp)
                    for c, (q, k) in enumerate(((qk_hi, k_hi), (qk_hi, k_lo), (qk_lo, k_hi), (qk_lo, k_lo))):
                        d = slice(HD * c, HD * c + HD)
                        sp.dma_start(q_stack[d, s, :].bitcast(F32), q[r, g, :].bitcast(F32)).then_inc(stacked[s], 16)
                        sp.dma_start(k_stack[d, s, :].bitcast(F32), k[r, g, :].bitcast(F32)).then_inc(stacked[s], 16)

                if not last:
                    sp.wait_ge(x_ready, at(t, N_x, 8))
                    unregistered(sp)
                    load_x(t + 1)
                    load_mask(t + 1)
                for h in range(H):
                    stack(h)
                if not last:
                    sp.wait_ge(biased, at(t, 32, 32))
                    unregistered(sp)
                    load_adj(t + 1)
                    sp.wait_ge(T_hi_ready, at(t, N_T, 8))
                    unregistered(sp)
                    sp.wait_ge(T_lo_ready, at(t, N_T, 8))
                    unregistered(sp)
                    load_adjT(t + 1)
                sp.wait_ge(x_ready, at(t, N_x, 16))
                unregistered(sp)
                sp.dma_start(out[bass.ds(t, 1)].rearrange(rows, p=P), x_sb[:, :, :]).then_inc(out_stored, 16)

            load_x(0)
            load_mask(0)
            load_adjT(0)
            load_adj(0)
            batch(0, False)
            with sp.Fori(1, B - 1) as t:
                batch(t, False)
            batch(B - 1, True)
            sp.wait_ge(out_stored, 16 * B)

        N_W = 16 * 16

        @block.gpsimd
        def _(pool):
            step = [0]

            def done(ins):
                step[0] += 1
                ins.then_inc(setup_pool, 1)
                pool.wait_ge(setup_pool, step[0])

            done(pool.memset(ident[:, :], 0.0))
            done(pool.affine_select(out=ident[:, :], in_=ident[:, :], compare_op=ALU.not_equal, fill=1.0,
                                    base=0, pattern=[[-1, P]], channel_multiplier=1))
            for c, v in ((k_rms, F * RMS_EPS), (k_ln, LN_EPS), (k_mhalf, -0.5), (k_deg, DEG_EPS), (k_neg1, -1.0)):
                done(pool.memset(c, v))
            pool.wait_ge(setup_dve, SETUP_DVE)

            def wide(c, n):
                return c.to_broadcast([P, n])

            def batch(t):
                k = [0]

                def stepped(ins):
                    k[0] += 1
                    ins.then_inc(pool_step, 1)
                    pool.wait_ge(pool_step, at(t, N_pool, k[0]))

                def layernorm(l):
                    pool.wait_ge(means, at(t, N_means, 4 * l + 4))
                    if l or later(t):
                        pool.wait_ge(h_ready, at(t, N_h, 4 * l))
                    if l == 0:
                        if later(t):
                            pool.wait_ge(h_hi_ready, at(t, 4, 0))
                    stepped(pool.tensor_tensor(ve, mv[:, :, 1], wide(k_ln, NT), ALU.add))
                    stepped(pool.tensor_tensor(rstd, ve, wide(k_mhalf, NT), ALU.pow))
                    stepped(pool.tensor_tensor(nmean, mv[:, :, 0], wide(k_neg1, NT), ALU.mult))
                    pool.tensor_tensor(nb, nmean, rstd, ALU.mult).then_inc(normed, 1)

                layernorm(0)
                pool.wait_ge(h_ready, at(t, N_h, 4))
                pool.wait_ge(h_hi_ready, at(t, 4, 4))
                for n in range(NT):
                    ins = pool.tensor_tensor(x_in[:, n, :], x_in[:, n, :], b2_b[:, :], ALU.add)
                ins.then_inc(xb2_ready, 1)
                for n in range(NT):
                    pool.wait_ge(squared, at(t, 8, 2 * n + 2))
                    stepped(pool.tensor_tensor(sse[:, n:n + 1], ss[:, n, 0:1], ss[:, n, 1:2], ALU.add))
                    pool.tensor_tensor(sse[:, n:n + 1], sse[:, n:n + 1], k_rms, ALU.add).then_inc(rms_eps, 1)
                    pool.wait_ge(rms_eps, at(t, 4, n + 1))
                    pool.tensor_tensor(rms[:, n:n + 1], sse[:, n:n + 1], k_mhalf, ALU.pow).then_inc(rms_ready, 1)
                pool.wait_ge(deg_ready, at(t, 1, 1))
                if later(t):
                    pool.wait_ge(x_ready, at(t, N_x, 0))
                stepped(pool.tensor_tensor(dege, deg, wide(k_deg, NT), ALU.add))
                pool.tensor_tensor(dinv, dege, wide(k_mhalf, NT), ALU.pow).then_inc(dinv_ready, 1)
                layernorm(1)
                layernorm(2)
                for g in range(2):
                    pool.wait_ge(inv_ready, at(t, 2, g + 1))
                    if g == 0:
                        if later(t):
                            pool.wait_ge(tp_full, at(t, N_tp, 0))
                    else:
                        pool.wait_ge(tp_full, at(t, N_tp, tp_of_inv[0] + 1))
                    for n in range(NT):
                        ins = pool.tensor_tensor(inv_x[:, n, :, :],
                                                 pinv[:, HG * g:HG * g + HG, n].unsqueeze(2).to_broadcast([P, HG, HD]),
                                                 one_b.unsqueeze(2).to_broadcast([P, HG, HD]), ALU.mult)
                    ins.then_inc(invx_ready, 1)
                layernorm(3)
                pool.wait_ge(h_ready, at(t, N_h, 16))
                for n in range(NT):
                    ins = pool.tensor_tensor(x_sb[:, n, :], x_sb[:, n, :], b3_b[:, :], ALU.add)
                ins.then_inc(xb3_ready, 1)
                assert k[0] == N_pool

            batch(0)
            with pool.Fori(1, B) as t:
                batch(t)

        @block.scalar
        def _(act):
            act.wait_ge(w_loaded, N_W)

            def hi(dst, src):
                return act.activation(dst, src, ACT.Identity)

            hi(w1_hi[:, :, :], big[:, 0:2048].rearrange("p (k n) -> p k n", k=DT)).then_inc(setup_act, 1)
            hi(w2_hi[:, :, :], big[:, 2048:4096].rearrange("p (k n) -> p k n", k=FT)).then_inc(setup_act, 1)
            hi(ws_hi[:, :, :, :].rearrange("p a k n -> p (a k n)"), big[:, 4096:6656]).then_inc(setup_act, 1)
            hi(wl_hi[:, :, 0:D], big[:, 6656:7168].rearrange("p (k n) -> p k n", k=DT)).then_inc(setup_act, 1)
            act.wait_ge(setup_dve, SETUP_DVE)

            def batch(t):
                def layernorm(l):
                    act.wait_ge(normed, at(t, N_normed, l + 1))
                    src = x_in if l == 0 else x_sb
                    if l == 0:
                        if later(t):
                            act.wait_ge(y_ps, at(t, N_y, 0))
                    for n in range(NT):
                        act.activation(h_f32[:, n, :], src[:, n, :], ACT.Relu, bias=nb[:, n:n + 1],
                                       scale=rstd[:, n:n + 1]).then_inc(h_ready, 1)
                        if l == 0:
                            act.activation(rows_hi[:, n, 0:D], src[:, n, :], ACT.Relu, bias=nb[:, n:n + 1],
                                           scale=rstd[:, n:n + 1]).then_inc(h_hi_ready, 1)

                def turned_hi(l, first):
                    for d in range(DT):
                        act.wait_ge(tp_full, at(t, N_tp, first + d + 1))
                        hi(T_hi[:, d, :], tp[(first + d) % 2][:, :]).then_inc(T_hi_ready, 1)

                act.wait_ge(adjT_loaded, at(t, 16, 16))
                if later(t):
                    act.wait_ge(y_ps, at(t, N_y, 0))
                hi(aT_hi[:, :, :], adjT_sb[:, :, :]).then_inc(aT_hi_ready, 1)
                act.wait_ge(diag_ready, at(t, 1, 1))
                act.wait_ge(aT_hi_ready, at(t, N_aT, 1))
                act.wait_ge(aT_lo_ready, at(t, N_aT, 1))
                hi(diag_of(aT_hi), diag).then_inc(aT_hi_ready, 1)
                layernorm(0)
                for d in range(DT):
                    act.wait_ge(agg_ps, at(t, 2, d + 1))
                    hi(T_hi[:, d, :], mm[d][:, :]).then_inc(T_hi_ready, 1)
                act.wait_ge(aT_hi_ready, at(t, N_aT, 2))
                act.wait_ge(aT_lo_ready, at(t, N_aT, 2))
                hi(diag_of(aT_hi), diag_of(adjT_sb)).then_inc(aT_hi_ready, 1)

                def square(n):
                    act.wait_ge(hid_ps, at(t, 4, n + 1))
                    for c in range(2):
                        if c == 0 and n == 0:
                            if later(t):
                                act.wait_ge(rms_ready, at(t, 4, 0))
                        if 2 * n + c >= 1:
                            act.wait_ge(squared, at(t, 8, 2 * n + c))
                        act.activation(junk[:, c, :], mm[2 + 2 * (n % 2) + c][:, :], ACT.Square,
                                       accum_out=ss[:, n, c:c + 1]).then_inc(squared, 1)

                square(0)
                for n in range(NT):
                    if n + 1 < NT:
                        square(n + 1)
                    act.wait_ge(hid_ready, at(t, 8, 2 * n + 2))
                    act.activation(hid[:, n % 2, :], hid[:, n % 2, :], ACT.Silu).then_inc(silu_done, 1)
                    for c in range(2):
                        k = 2 * n + c
                        act.wait_ge(tp_full, at(t, N_tp, k + 1))
                        if n >= 2:
                            act.wait_ge(y_ps, at(t, N_y, n - 1))
                        hi(s_hi[:, n % 2, 4 * c:4 * c + 4, :].rearrange("p f n -> p (f n)"),
                           tp[k % 2][:, :]).then_inc(s_hi_ready, 1)

                layernorm(1)
                turned_hi(1, 8)
                for n in range(NT):
                    act.wait_ge(lin_ps, at(t, 4, n + 1))
                    hi(rows_hi[:, n, 0:D], mm[n][:, 0:D]).then_inc(lin_hi_ready, 1)
                act.wait_ge(s1_ps, at(t, 1, 1))
                for m in range(NT):
                    act.wait_ge(s2_ready, at(t, 4, m + 1))
                    if m >= 2:
                        act.wait_ge(att_ready, at(t, 4, m - 1))
                    act.activation(sig[:, m % 2, :], mm[4][:, :], ACT.Sigmoid, bias=s2[:, m:m + 1]).then_inc(sig_ready, 1)
                for m in range(NT):
                    act.wait_ge(att_ready, at(t, 4, m + 1))
                    hi(att_hi[:, m, :], att[:, m % 2, :]).then_inc(att_hi_ready, 1)

                layernorm(2)
                turned_hi(2, 10)
                for g in range(DT):
                    act.wait_ge(qk_ps, at(t, 4, 2 * g + 1))
                    act.activation(qk_hi[:, g, :], mm[2 * g][:, :], ACT.Identity,
                                   scale=q_scale[:, g:g + 1]).then_inc(qk_hi_ready, 1)
                    act.wait_ge(qk_ps, at(t, 4, 2 * g + 2))
                    hi(k_hi[:, g, :], mm[2 * g + 1][:, :]).then_inc(qk_hi_ready, 1)
                for j in range(2):
                    act.wait_ge(v_ps, at(t, 2, j + 1))
                    act.activation(vals[:, 2 * j:2 * j + 2, :].rearrange("p a d -> p (a d)"), mm[4 + j][:, :],
                                   ACT.Copy).then_inc(v_ready, 1)

                def exps(h):
                    for n in range(NT):
                        i = 4 * h + n
                        act.wait_ge(biased, at(t, 32, i + 1))
                        act.activation(prob[:, i % 6, :], prob[:, i % 6, :], ACT.Exp, bias=nmax[:, h, n:n + 1],
                                       scale=-1.0, accum_out=psum_[:, h, n:n + 1]).then_inc(exped, 1)

                def turned_probs(h):
                    if h == HG:
                        act.wait_ge(av_ps, at(t, 2, 1))
                    for j in range(3):
                        k = tp_of_prob[h, j]
                        act.wait_ge(tp_full, at(t, N_tp, k + 1))
                        act.activation(pT[:, h % HG, j, :], tp[k % 2][:, :], ACT.Copy).then_inc(pT_act, 1)

                exps(0)
                for h in range(H):
                    turned_probs(h)
                    if h + 1 < H:
                        exps(h + 1)
                    if h in (HG, H - 1):
                        g = 0 if h == HG else 1
                        act.wait_ge(o_ready, at(t, 2, g + 1))
                        hi(T_hi[:, g, :], o_f32[:, g, :]).then_inc(T_hi_ready, 1)

                layernorm(3)
                turned_hi(3, tp_of_L3)
                act.wait_ge(dinv_ready, at(t, 1, 1))
                for n in range(NT):
                    act.wait_ge(sup_ps, at(t, 4, n + 1))
                    act.activation(rows_hi[:, n, 0:D], mm[n][:, 0:D], ACT.Identity,
                                   scale=dinv[:, n:n + 1]).then_inc(sup_hi_ready, 1)

            batch(0)
            with act.Fori(1, B) as t:
                batch(t)

        @block.vector
        def _(dve):
            step = [0]

            def done(ins):
                step[0] += 1
                ins.then_inc(setup_dve, 1)
                dve.wait_ge(setup_dve, step[0])

            for tile in (b1_rows, ones_rows):
                done(dve.memset(tile[:, :].bitcast(F32), 0.0))
            for r in (0, 32):
                done(dve.memset(ones_rows[r:r + 1, :].bitcast(F32), 1.0))
            done(dve.memset(k_zero, 0.0))
            done(dve.memset(one_b, 1.0))
            dve.wait_ge(w_loaded, N_W)
            b1_stage = prob[:, 0:2, :].rearrange("p a n -> p (a n)")
            for r in (0, 32):
                done(dve.tensor_copy(b1_rows[r:r + 1, :], b1_stage[r:r + 1, :]))
            done(dve.tensor_tensor(b1_rows[32:33, :], b1_stage[32:33, :], b1_rows[32:33, :].bitcast(F32), ALU.subtract))
            done(dve.tensor_scalar(rmsw_b[:, :], rmsw_b[:, :], float(F) ** 0.5, None, ALU.mult))
            for w, sgn, mag in ((cst[:, 8:16], t8, t8b), (cst[:, 6:8], t2, t2b)):
                done(dve.tensor_scalar(sgn, w, 0.0, 2.0, ALU.is_ge, ALU.mult))
                done(dve.tensor_scalar(sgn, sgn, 1.0, None, ALU.subtract))
                done(dve.tensor_tensor(mag, w, sgn, ALU.mult))
                done(dve.tensor_scalar(mag, mag, TINY, None, ALU.max))
            done(dve.scalar_tensor_tensor(out=neg_w, in0=t8b, scalar=-1.0, in1=t8, op0=ALU.mult, op1=ALU.mult))
            done(dve.scalar_tensor_tensor(out=t2c, in0=t2b, scalar=HD ** 0.5, in1=t2, op0=ALU.mult, op1=ALU.mult))
            done(dve.reciprocal(q_scale, t2c))
            dve.wait_ge(setup_pool, 7)
            for h in range(H):
                done(dve.tensor_scalar(neg_mask[:, h, :], ident[:, :], t8[:, h:h + 1], -BIG, ALU.mult, ALU.mult))
            dve.wait_ge(setup_act, 4)

            def lo(dst, src, high):
                return dve.tensor_tensor(dst, src, high.bitcast(F32), ALU.subtract)

            done(lo(w1_lo[:, :, :], big[:, 0:2048].rearrange("p (k n) -> p k n", k=DT), w1_hi[:, :, :]))
            done(lo(w2_lo[:, :, :], big[:, 2048:4096].rearrange("p (k n) -> p k n", k=FT), w2_hi[:, :, :]))
            done(lo(ws_lo[:, :, :, :].rearrange("p a k n -> p (a k n)"), big[:, 4096:6656],
                    ws_hi[:, :, :, :].rearrange("p a k n -> p (a k n)")))
            done(lo(wl_lo[:, :, 0:D], big[:, 6656:7168].rearrange("p (k n) -> p k n", k=DT), wl_hi[:, :, 0:D]))
            dve.wait_ge(setup_pe, 1)
            for k in range(DT):
                src = mm[k][:, 0:2]
                done(dve.tensor_copy(wl_hi[:, k, D:DE], src))
                done(lo(wl_lo[:, k, D:DE], src, wl_hi[:, k, D:DE]))
                for w, e in ((wa_hi, wl_hi), (wa_lo, wl_lo)):
                    done(dve.tensor_copy(w[:, k, :], e[:, k, D + 1:D + 2].bitcast(F32).to_broadcast([P, P])))
            done(dve.tensor_copy(t2, mm[2][:, 0:2]))
            done(dve.tensor_scalar(s_const, t2[:, 0:1], t2[:, 1:2], cst[:, 17:18], ALU.add, ALU.add))
            assert step[0] == SETUP_DVE, step[0]

            def batch(t):
                def layernorm(l):
                    src = x_in if l == 0 else x_sb
                    if l == 0:
                        dve.wait_ge(x_loaded, at(t, 16, 16))
                    else:
                        dve.wait_ge(x_ready, at(t, N_x, 4 * l))
                    for n in range(NT):
                        if n == 0:
                            if l or later(t):
                                dve.wait_ge(normed, at(t, N_normed, l))
                        dve.bn_stats(bn[:, n, :], src[:, n, :]).then_inc(stats, 1)
                    dve.wait_ge(stats, at(t, N_stats, 4 * l + 4))
                    dve.memset(fence, 0.0).then_inc(fenced, 1)
                    for n in range(NT):
                        dve.bn_aggr(mv[:, n, :], bn[:, n, :]).then_inc(means, 1)

                def turned_lo(l, first):
                    i = {1: 2, 2: 4, 3: 8}[l]
                    for d in range(DT):
                        dve.wait_ge(T_hi_ready, at(t, N_T, i + d + 1))
                        lo(T_lo[:, d, :], tp[(first + d) % 2][:, :], T_hi[:, d, :]).then_inc(T_lo_ready, 1)

                dve.wait_ge(aT_hi_ready, at(t, N_aT, 1))
                lo(aT_lo[:, :, :], adjT_sb[:, :, :], aT_hi[:, :, :]).then_inc(aT_lo_ready, 1)
                dve.scalar_tensor_tensor(out=diag, in0=ident[:, :].unsqueeze(1).to_broadcast([P, NT, P]),
                                         scalar=cst[:, 16:17], in1=diag_of(adjT_sb),
                                         op0=ALU.mult, op1=ALU.add).then_inc(diag_ready, 1)
                layernorm(0)
                dve.wait_ge(aT_hi_ready, at(t, N_aT, 2))
                dve.wait_ge(aT_lo_ready, at(t, N_aT, 1))
                lo(diag_of(aT_lo), diag, diag_of(aT_hi)).then_inc(aT_lo_ready, 1)
                for n in range(NT):
                    dve.wait_ge(h_hi_ready, at(t, 4, n + 1))
                    lo(rows_lo[:, n, 0:D], h_f32[:, n, :], rows_hi[:, n, 0:D]).then_inc(h_lo_ready, 1)
                for d in range(DT):
                    dve.wait_ge(T_hi_ready, at(t, N_T, d + 1))
                    lo(T_lo[:, d, :], mm[d][:, :], T_hi[:, d, :]).then_inc(T_lo_ready, 1)
                dve.wait_ge(aT_hi_ready, at(t, N_aT, 3))
                dve.wait_ge(aT_lo_ready, at(t, N_aT, 2))
                lo(diag_of(aT_lo), diag_of(adjT_sb), diag_of(aT_hi)).then_inc(aT_lo_ready, 1)
                dve.wait_ge(adj_loaded, at(t, 16, 16))
                if later(t):
                    dve.wait_ge(sc_ps, at(t, 32, 0))
                dve.tensor_scalar(unlinked[:, :, :], adj_sb[:, :, :], 0.0, None, ALU.is_equal).then_inc(unlinked_ready, 1)
                if later(t):
                    dve.wait_ge(dinv_ready, at(t, 1, 0))
                dve.tensor_reduce(deg, adj_sb[:, :, :], AX.X, ALU.add).then_inc(deg_ready, 1)

                def hidden(n):
                    dve.wait_ge(rms_ready, at(t, 4, n + 1))
                    if n >= 2:
                        dve.wait_ge(tp_full, at(t, N_tp, 2 * (n - 2) + 2))
                    for c in range(2):
                        dve.scalar_tensor_tensor(out=hid[:, n % 2, N * c:N * c + N], in0=mm[2 + 2 * (n % 2) + c][:, :],
                                                 scalar=rms[:, n:n + 1], in1=rmsw_b[:, N * c:N * c + N],
                                                 op0=ALU.mult, op1=ALU.mult).then_inc(hid_ready, 1)

                def hidden_lo(n):
                    for c in range(2):
                        k = 2 * n + c
                        dve.wait_ge(s_hi_ready, at(t, 8, k + 1))
                        f = slice(4 * c, 4 * c + 4)
                        lo(s_lo[:, n % 2, f, :].rearrange("p f n -> p (f n)"), tp[k % 2][:, :],
                           s_hi[:, n % 2, f, :].rearrange("p f n -> p (f n)")).then_inc(s_lo_ready, 1)

                def update0(n):
                    dve.wait_ge(y_ps, at(t, N_y, n + 1))
                    if n == 0:
                        dve.wait_ge(xb2_ready, at(t, 1, 1))
                        if later(t):
                            dve.wait_ge(out_stored, t * 16)
                    dve.tensor_tensor(x_sb[:, n, :], mm[n % 2][:, 0:D], x_in[:, n, :], ALU.add).then_inc(x_ready, 1)

                hidden(0)
                hidden(1)
                hidden_lo(0)
                hidden(2)
                update0(0)
                hidden_lo(1)
                hidden(3)
                update0(1)
                hidden_lo(2)
                hidden_lo(3)
                update0(2)
                update0(3)

                layernorm(1)
                turned_lo(1, 8)
                for n in range(NT):
                    dve.wait_ge(lin_hi_ready, at(t, 4, n + 1))
                    lo(rows_lo[:, n, 0:D], mm[n][:, 0:D], rows_hi[:, n, 0:D]).then_inc(lin_lo_ready, 1)
                    if n == 0:
                        if later(t):
                            dve.wait_ge(sig_ready, at(t, 4, 0))
                    dve.tensor_scalar(s2[:, n:n + 1], mm[n][:, D:D + 1], s_const, None, ALU.add).then_inc(s2_ready, 1)
                dve.memset(rows_hi[:, :, D:D + 1].bitcast(F32), 1.0)
                dve.memset(rows_hi[:, :, D + 1:DE].bitcast(F32), 0.0)
                dve.memset(rows_lo[:, :, D:DE].bitcast(F32), 0.0).then_inc(ones_ready, 1)
                dve.wait_ge(mask_loaded, at(t, 16, 16))
                for m in range(NT):
                    dve.wait_ge(sig_ready, at(t, 4, m + 1))
                    if m >= 2:
                        dve.wait_ge(att_hi_ready, at(t, 4, m - 1))
                        dve.wait_ge(att_lo_ready, at(t, 4, m - 1))
                    dve.scalar_tensor_tensor(out=att[:, m % 2, :], in0=sig[:, m % 2, :], scalar=mask_sb[:, m:m + 1],
                                             in1=adjT_sb[:, m, :], op0=ALU.mult, op1=ALU.mult).then_inc(att_ready, 1)
                    if m >= 1:
                        dve.wait_ge(att_hi_ready, at(t, 4, m))
                        lo(att_lo[:, m - 1, :], att[:, (m - 1) % 2, :], att_hi[:, m - 1, :]).then_inc(att_lo_ready, 1)
                dve.wait_ge(att_hi_ready, at(t, 4, NT))
                lo(att_lo[:, NT - 1, :], att[:, (NT - 1) % 2, :], att_hi[:, NT - 1, :]).then_inc(att_lo_ready, 1)
                u = [0]

                def upd(ins):
                    u[0] += 1
                    ins.then_inc(upd_step, 1)
                    dve.wait_ge(upd_step, at(t, 16, u[0]))

                for n in range(NT):
                    c = slice(n, n + 1)
                    dve.wait_ge(y_ps, at(t, N_y, 4 + n + 1))
                    upd(dve.tensor_scalar(den[:, c], mm[n][:, D:D + 1], mask_sb[:, c], ATT_EPS, ALU.mult, ALU.add))
                    upd(dve.reciprocal(rec[:, c], den[:, c]))
                    upd(dve.tensor_scalar(fac[:, c], rec[:, c], mask_sb[:, c], mask_sb[:, c], ALU.mult, ALU.mult))
                    dve.tensor_copy(small[:, 204 + n:205 + n], mm[n][:, D:D + 1]).then_inc(rowsum_ready, 1)
                    dve.wait_ge(rowsum_ready, at(t, 4, n + 1))
                    upd(dve.scalar_tensor_tensor(out=msg[:, n, :], in0=bL_b[:, :], scalar=small[:, 204 + n:205 + n],
                                                 in1=mm[n][:, 0:D], op0=ALU.mult, op1=ALU.add))
                    dve.scalar_tensor_tensor(out=x_sb[:, n, :], in0=msg[:, n, :], scalar=fac[:, c], in1=x_sb[:, n, :],
                                             op0=ALU.mult, op1=ALU.add).then_inc(x_ready, 1)

                layernorm(2)
                turned_lo(2, 10)
                for g in range(DT):
                    dve.wait_ge(qk_hi_ready, at(t, 4, 2 * g + 1))
                    dve.scalar_tensor_tensor(out=qk_lo[:, g, :], in0=mm[2 * g][:, :], scalar=q_scale[:, g:g + 1],
                                             in1=qk_hi[:, g, :].bitcast(F32), op0=ALU.mult,
                                             op1=ALU.subtract).then_inc(qk_lo_ready, 1)
                    dve.wait_ge(qk_hi_ready, at(t, 4, 2 * g + 2))
                    lo(k_lo[:, g, :], mm[2 * g + 1][:, :], k_hi[:, g, :]).then_inc(qk_lo_ready, 1)

                def bias(h):
                    for n in range(NT):
                        i = 4 * h + n
                        dve.wait_ge(sc_ps, at(t, 32, i + 1))
                        if i >= 6:
                            dve.wait_ge(tp_full, at(t, N_tp, tp_of_prob[(i - 6) // 4, NT - 1] + 1))
                        unregistered(dve)
                        dve.tensor_tensor_reduce(out=prob[:, i % 6, :], in0=mm[n][:, :], in1=adj_sb[:, n, :],
                                                 scale=neg_w[:, h:h + 1], scalar=3e38, op0=ALU.add, op1=ALU.min,
                                                 accum_out=nmax[:, h, n:n + 1]).then_inc(biased, 1)

                def turned_probs(h):
                    if h == HG:
                        dve.wait_ge(av_ps, at(t, 2, 1))
                    k = tp_of_prob[h, 3]
                    dve.wait_ge(tp_full, at(t, N_tp, k + 1))
                    dve.tensor_copy(pT[:, h % HG, 3, :], tp[k % 2][:, :]).then_inc(pT_dve, 1)

                def inverse(g):
                    dve.wait_ge(exped, at(t, 32, 16 * g + 16))
                    dve.reciprocal(pinv[:, HG * g:HG * g + HG, :].rearrange("p h n -> p (h n)"),
                                   psum_[:, HG * g:HG * g + HG, :].rearrange("p h n -> p (h n)")).then_inc(inv_ready, 1)

                def attended(g):
                    k = tp_of_inv[g]
                    dve.wait_ge(tp_full, at(t, N_tp, k + 1))
                    dve.tensor_copy(o_f32[:, g, :], tp[k % 2][:, :]).then_inc(lb_ready, 1)
                    dve.wait_ge(lb_ready, at(t, 2, g + 1))
                    dve.wait_ge(av_ps, at(t, 2, g + 1))
                    dve.tensor_tensor(o_f32[:, g, :], mm[4 + g][:, :], o_f32[:, g, :], ALU.mult).then_inc(o_ready, 1)
                    dve.wait_ge(T_hi_ready, at(t, N_T, 6 + g + 1))
                    lo(T_lo[:, g, :], o_f32[:, g, :], T_hi[:, g, :]).then_inc(T_lo_ready, 1)

                bias(0)
                for h in range(H):
                    if h + 1 < H:
                        bias(h + 1)
                    turned_probs(h)
                    if h == HG - 1:
                        inverse(0)
                    if h == HG:
                        attended(0)
                    if h == H - 1:
                        inverse(1)
                        attended(1)

                for n in range(NT):
                    dve.wait_ge(y_ps, at(t, N_y, 8 + n + 1))
                    dve.tensor_tensor(x_sb[:, n, :], mm[n][:, 0:D], x_sb[:, n, :], ALU.add).then_inc(x_ready, 1)

                layernorm(3)
                turned_lo(3, tp_of_L3)
                dve.wait_ge(dinv_ready, at(t, 1, 1))
                for n in range(NT):
                    dve.wait_ge(sup_hi_ready, at(t, 4, n + 1))
                    dve.scalar_tensor_tensor(out=rows_lo[:, n, 0:D], in0=mm[n][:, 0:D], scalar=dinv[:, n:n + 1],
                                             in1=rows_hi[:, n, 0:D].bitcast(F32), op0=ALU.mult,
                                             op1=ALU.subtract).then_inc(sup_lo_ready, 1)
                dve.wait_ge(xb3_ready, at(t, 1, 1))
                for n in range(NT):
                    dve.wait_ge(y_ps, at(t, N_y, 12 + n + 1))
                    dve.scalar_tensor_tensor(out=x_sb[:, n, :], in0=mm[n][:, 0:D], scalar=dinv[:, n:n + 1],
                                             in1=x_sb[:, n, :], op0=ALU.mult, op1=ALU.add).then_inc(x_ready, 1)

            batch(0)
            with dve.Fori(1, B) as t:
                batch(t)

        @block.tensor
        def _(pe):
            def product(ps, a, b, start, stop):
                pe.matmul(ps, a[0], b[0], start=start, stop=False)
                pe.matmul(ps, a[0], b[1], start=False, stop=False)
                return pe.matmul(ps, a[1], b[0], start=False, stop=stop)

            pe.wait_ge(w_loaded, N_W)
            wln = big[:, 7168:7680].rearrange("p (k n) -> p k n", k=DT)
            for i in range(DT):
                for k in range(DT):
                    pe.matmul(mm[i][:, 0:2], wln[:, k, P * i:P * i + P], cst[:, 2 * k:2 * k + 2],
                              start=(k == 0), stop=(k == DT - 1))
            for k in range(DT):
                last = pe.matmul(mm[2][:, 0:2], cst[:, 4 + k:5 + k].to_broadcast([P, P]), cst[:, 2 * k:2 * k + 2],
                                 start=(k == 0), stop=(k == DT - 1))
            last.then_inc(setup_pe, 1)
            pe.wait_ge(setup_dve, SETUP_DVE)

            def batch(t):
                def turn_h(l, first):
                    for d in range(DT):
                        wait_tp_free(pe, t, first + d)
                        if d == 0:
                            pe.wait_ge(h_ready, at(t, N_h, 4 * l + 4))
                        for n in range(NT):
                            last = pe.transpose(tp[(first + d) % 2][:, P * n:P * n + P],
                                                h_f32[:, n, P * d:P * d + P], ident[:, :])
                        last.then_inc(tp_full, 1)

                def both(hi_, lo_, *ix):
                    return hi_[ix], lo_[ix]

                A = slice(None)
                pe.wait_ge(h_hi_ready, at(t, 4, 4))
                pe.wait_ge(h_lo_ready, at(t, 4, 4))
                pe.wait_ge(aT_hi_ready, at(t, N_aT, 2))
                pe.wait_ge(aT_lo_ready, at(t, N_aT, 2))
                if later(t):
                    pe.wait_ge(x_ready, at(t, N_x, 0))
                for d in range(DT):
                    for m in range(NT):
                        last = product(mm[d][:, :], both(rows_hi, rows_lo, A, m, slice(P * d, P * d + P)),
                                       both(aT_hi, aT_lo, A, m, A), m == 0, m == NT - 1)
                    last.then_inc(agg_ps, 1)

                def hidden(n):
                    if n == 0:
                        pe.wait_ge(T_hi_ready, at(t, N_T, 2))
                        pe.wait_ge(T_lo_ready, at(t, N_T, 2))
                    if n >= 2:
                        pe.wait_ge(hid_ready, at(t, 8, 2 * (n - 2) + 2))
                    for c in range(2):
                        ps = mm[2 + 2 * (n % 2) + c][:, :]
                        cs = slice(N * c, N * c + N)
                        pe.matmul(ps, ones_rows[:, :], b1_rows[:, cs], start=True, stop=False)
                        for k in range(DT):
                            last = product(ps, both(T_hi, T_lo, A, k, slice(P * n, P * n + P)),
                                           both(w1_hi, w1_lo, A, k, cs), False, k == DT - 1)
                    last.then_inc(hid_ps, 1)

                def turn_hidden(n):
                    pe.wait_ge(silu_done, at(t, 4, n + 1))
                    for c in range(2):
                        k = 2 * n + c
                        wait_tp_free(pe, t, k)
                        for f in range(4):
                            last = pe.transpose(tp[k % 2][:, P * f:P * f + P],
                                                hid[:, n % 2, P * (4 * c + f):P * (4 * c + f) + P], ident[:, :])
                        last.then_inc(tp_full, 1)

                def down(n):
                    pe.wait_ge(s_hi_ready, at(t, 8, 2 * n + 2))
                    pe.wait_ge(s_lo_ready, at(t, 8, 2 * n + 2))
                    if n >= 2:
                        pe.wait_ge(x_ready, at(t, N_x, n - 1))
                    for f in range(FT):
                        last = product(mm[n % 2][:, 0:D], both(s_hi, s_lo, A, n % 2, f, A),
                                       both(w2_hi, w2_lo, A, f, A), f == 0, f == FT - 1)
                    last.then_inc(y_ps, 1)

                hidden(0)
                hidden(1)
                turn_hidden(0)
                hidden(2)
                down(0)
                turn_hidden(1)
                hidden(3)
                down(1)
                turn_hidden(2)
                turn_hidden(3)
                down(2)
                down(3)

                turn_h(1, 8)
                pe.wait_ge(T_hi_ready, at(t, N_T, 4))
                pe.wait_ge(T_lo_ready, at(t, N_T, 4))
                for n in range(NT):
                    for k in range(DT):
                        last = product(mm[n][:, 0:DE], both(T_hi, T_lo, A, k, slice(P * n, P * n + P)),
                                       both(wl_hi, wl_lo, A, k, A), k == 0, k == DT - 1)
                    last.then_inc(lin_ps, 1)
                for k in range(DT):
                    last = product(mm[4][:, :], both(wa_hi, wa_lo, A, k, A), both(T_hi, T_lo, A, k, A),
                                   k == 0, k == DT - 1)
                last.then_inc(s1_ps, 1)
                pe.wait_ge(lin_hi_ready, at(t, 4, 4))
                pe.wait_ge(lin_lo_ready, at(t, 4, 4))
                pe.wait_ge(s2_ready, at(t, 4, 4))
                pe.wait_ge(ones_ready, at(t, 1, 1))
                for m in range(NT):
                    pe.wait_ge(att_hi_ready, at(t, 4, m + 1))
                    pe.wait_ge(att_lo_ready, at(t, 4, m + 1))
                    for n in range(NT):
                        last = product(mm[n][:, 0:DE], both(att_hi, att_lo, A, m, slice(P * n, P * n + P)),
                                       both(rows_hi, rows_lo, A, m, A), m == 0, m == NT - 1)
                        if m == NT - 1:
                            last.then_inc(y_ps, 1)

                turn_h(2, 10)
                pe.wait_ge(T_hi_ready, at(t, N_T, 6))
                pe.wait_ge(T_lo_ready, at(t, N_T, 6))
                for g in range(DT):
                    for i, w in enumerate((WQ, WK)):
                        for k in range(DT):
                            last = product(mm[2 * g + i][:, :], both(ws_hi, ws_lo, A, w, k, slice(P * g, P * g + P)),
                                           both(T_hi, T_lo, A, k, A), k == 0, k == DT - 1)
                        last.then_inc(qk_ps, 1)
                for n in range(NT):
                    for k in range(DT):
                        last = product(mm[4 + n // 2][:, D * (n % 2):D * (n % 2) + D],
                                       both(T_hi, T_lo, A, k, slice(P * n, P * n + P)),
                                       both(ws_hi, ws_lo, A, WV, k, A), k == 0, k == DT - 1)
                    if n % 2:
                        last.then_inc(v_ps, 1)

                def scores(h):
                    pe.wait_ge(stacked[h % 4], at(t, 2 * 128, 128 * (h // 4 + 1)))
                    if h == 0:
                        pe.wait_ge(unlinked_ready, at(t, 1, 1))
                        pe.wait_ge(qk_lo_ready, at(t, 4, 4))
                    for n in range(NT):
                        if h:
                            pe.wait_ge(biased, at(t, 32, 4 * (h - 1) + n + 1))
                        pe.matmul(mm[n][:, :], q_stack[:, h % 4, P * n:P * n + P], k_stack[:, h % 4, :],
                                  start=True, stop=False)
                        pe.matmul(mm[n][:, :], neg_mask[:, h, :], unlinked[:, n, :],
                                  start=False, stop=True).then_inc(sc_ps, 1)

                def turn_probs(h):
                    pe.wait_ge(exped, at(t, 32, 4 * h + 4))
                    for j in range(NT):
                        k = tp_of_prob[h, j]
                        wait_tp_free(pe, t, k)
                        for n in range(NT):
                            last = pe.transpose(tp[k % 2][:, P * n:P * n + P],
                                                prob[:, (4 * h + n) % 6, P * j:P * j + P], ident[:, :])
                        last.then_inc(tp_full, 1)

                def attend(g):
                    pe.wait_ge(v_ready, at(t, 2, 2))
                    pe.wait_ge(pT_act, at(t, 24, 12 * g + 12))
                    pe.wait_ge(pT_dve, at(t, 8, 4 * g + 4))
                    for j in range(NT):
                        for h in range(HG):
                            last = pe.matmul(mm[4 + g][HD * h:HD * h + HD, :],
                                             vals[:, j, P * g + HD * h:P * g + HD * h + HD], pT[:, h, j, :],
                                             start=(j == 0), stop=(j == NT - 1), tile_position=(0, HD * h))
                    last.then_inc(av_ps, 1)

                def turn_inverse(g):
                    pe.wait_ge(invx_ready, at(t, 2, g + 1))
                    k = tp_of_inv[g]
                    wait_tp_free(pe, t, k)
                    for n in range(NT):
                        last = pe.transpose(tp[k % 2][:, P * n:P * n + P],
                                            inv_x[:, n, :, :].rearrange("p h d -> p (h d)"), ident[:, :])
                    last.then_inc(tp_full, 1)

                scores(0)
                for h in range(H):
                    if h + 1 < H:
                        scores(h + 1)
                    turn_probs(h)
                    if h == HG - 1:
                        attend(0)
                    if h == HG:
                        turn_inverse(0)
                attend(1)
                turn_inverse(1)
                pe.wait_ge(T_hi_ready, at(t, N_T, 8))
                pe.wait_ge(T_lo_ready, at(t, N_T, 8))
                for n in range(NT):
                    for g in range(DT):
                        last = product(mm[n][:, 0:D], both(T_hi, T_lo, A, g, slice(P * n, P * n + P)),
                                       both(ws_hi, ws_lo, A, WO, g, A), g == 0, g == DT - 1)
                    last.then_inc(y_ps, 1)

                turn_h(3, tp_of_L3)
                pe.wait_ge(T_hi_ready, at(t, N_T, 10))
                pe.wait_ge(T_lo_ready, at(t, N_T, 10))
                for n in range(NT):
                    for k in range(DT):
                        last = product(mm[n][:, 0:D], both(T_hi, T_lo, A, k, slice(P * n, P * n + P)),
                                       both(ws_hi, ws_lo, A, WG, k, A), k == 0, k == DT - 1)
                    last.then_inc(sup_ps, 1)
                pe.wait_ge(aT_hi_ready, at(t, N_aT, 3))
                pe.wait_ge(aT_lo_ready, at(t, N_aT, 3))
                pe.wait_ge(sup_hi_ready, at(t, 4, 4))
                pe.wait_ge(sup_lo_ready, at(t, 4, 4))
                for n in range(NT):
                    for m in range(NT):
                        last = product(mm[n][:, 0:D], both(aT_hi, aT_lo, A, m, slice(P * n, P * n + P)),
                                       both(rows_hi, rows_lo, A, m, slice(0, D)), m == 0, m == NT - 1)
                    last.then_inc(y_ps, 1)

            batch(0)
            with pe.Fori(1, B) as t:
                batch(t)



def kernel(x, adj, nodemask, L0_gnn_epsilon, L0_gnn_W1, L0_gnn_b1, L0_gnn_rms_weight, L0_gnn_W2, L0_gnn_b2,
           L1_gnn_W, L1_gnn_b, L1_gnn_a1, L1_gnn_a2, L1_gnn_att_b, L2_gnn_W_q, L2_gnn_W_k, L2_gnn_W_v, L2_gnn_W_e,
           L2_gnn_W_o, L3_gnn_weight, L3_gnn_bias):
    import numpy as np
    import concourse.bacc as bacc
    from concourse.bass_utils import run_bass_kernel_spmd

    x, adj = np.asarray(x), np.asarray(adj)
    B, N, D = x.shape

    def rows(v, n):
        return np.asarray(v).reshape(n, P).T

    def wide(v, n):
        return np.broadcast_to(np.asarray(v).reshape(1, n), (P, n))

    a = np.stack([rows(L1_gnn_a2, 2), rows(L1_gnn_a1, 2)], axis=-1).reshape(P, 4)
    edge = np.asarray(L2_gnn_W_e).reshape(-1)
    cols = np.concatenate([a, rows(L1_gnn_b, 2), rows(np.repeat(edge, D // edge.size), 2), wide(edge, edge.size),
                           wide(L0_gnn_epsilon, 1), wide(L1_gnn_att_b, 1)], axis=1)
    arrays = {
        "x": x, "adj": adj, "adjT": adj.transpose(0, 2, 1),
        "maskT": np.asarray(nodemask).reshape(B, N // P, P).transpose(0, 2, 1),
        "W1": L0_gnn_W1, "b1": L0_gnn_b1, "rmsw": L0_gnn_rms_weight, "W2": L0_gnn_W2, "b2": L0_gnn_b2,
        "WL": np.asarray(L1_gnn_W).T, "WLn": L1_gnn_W, "bL": L1_gnn_b,
        "WqT": np.asarray(L2_gnn_W_q).T, "WkT": np.asarray(L2_gnn_W_k).T, "WvT": np.asarray(L2_gnn_W_v).T,
        "WoT": np.asarray(L2_gnn_W_o).T, "W3": L3_gnn_weight, "b3": L3_gnn_bias, "cols": cols,
    }
    nc = bacc.Bacc("TRN2", target_bir_lowering=False, num_devices=1)
    ins, args = {}, []
    for name, v in arrays.items():
        v = np.ascontiguousarray(v)
        ins[f"in_{name}"] = v
        args.append(nc.dram_tensor(f"in_{name}", v.shape, mybir.dt.from_np(v.dtype), kind="ExternalInput").ap())
    out = nc.dram_tensor("out", (B, N, D), F32, kind="ExternalOutput").ap()
    gnn_kernel(nc, *args, out)
    r = run_bass_kernel_spmd(nc, [ins], core_ids=[0])
    return r.results[0]["out"]
```

```python
from contextlib import ExitStack

import concourse.bass as bass
from concourse import mybir

ALU = mybir.AluOpType
ACT = mybir.ActivationFunctionType
AX = mybir.AxisListType
F32 = mybir.dt.float32
F32R = mybir.dt.float32r
BF16 = mybir.dt.bfloat16

P = 128
BIG = 1e37
TINY = 1e-20
LN_EPS, RMS_EPS, ATT_EPS, DEG_EPS = 1e-5, 1e-6, 1e-8, 1e-5


def at(t, per_batch, k):
    return t * per_batch + k


def later(t):
    return not isinstance(t, int) or t > 0


def gnn_kernel(nc, x, adj, adjT, maskT, W1, b1, rmsw, W2, b2, WL, WLn, bL, WqT, WkT, WvT, WoT, W3, b3, cols, out):
    B, N, D = x.shape
    H = 8
    HD = D // H
    F = W1.shape[1]
    NT, DT, FT = N // P, D // P, F // P
    HG = P // HD
    DE = D + 2
    A = slice(None)

    with ExitStack() as ctx:
        def sb(name, shape, dt=F32):
            return ctx.enter_context(nc.sbuf_tensor(name, shape, dt))

        def sem(name):
            return ctx.enter_context(nc.semaphore(name))

        w1_hi, w1_lo = (sb(f"w1_{s}", [P, DT, F], F32R) for s in ("hi", "lo"))
        w2_hi, w2_lo = (sb(f"w2_{s}", [P, FT, D], F32R) for s in ("hi", "lo"))
        ws = sb("ws", [P, 5, DT, D])
        WQ, WK, WV, WO, WG = range(5)
        wl = sb("wl", [P, DT, DE])
        wa = sb("wa", [P, DT, P])
        b1_rows = sb("b1_rows", [P, F], F32R)
        ones_rows = sb("ones_rows", [P, P], F32R)
        rmsw_b = sb("rmsw_b", [P, F])
        bL_b, b2_b, b3_b = sb("bL_b", [P, D]), sb("b2_b", [P, D]), sb("b3_b", [P, D])
        ident = sb("ident", [P, P])
        neg_mask = sb("neg_mask", [P, H, P], BF16)
        cst = sb("cst", [P, 18])
        drv = sb("drv", [P, 46])
        neg_w = drv[:, 0:8]
        q_scale = drv[:, 8:10]
        s_const = drv[:, 10:11]
        k_rms, k_ln, k_mhalf, k_deg, k_neg1 = (drv[:, 11 + i:12 + i] for i in range(5))
        one_b = drv[:, 41:45]
        t8, t8b = drv[:, 16:24], drv[:, 24:32]
        t2, t2b, t2c = drv[:, 32:34], drv[:, 34:36], drv[:, 36:38]

        x_in = sb("x_in", [P, NT, D])
        adjT_f = sb("adjT_f", [P, NT, N])
        hf = sb("hf", [P, NT, D])
        T_hi, T_lo = (sb(f"T_{s}", [P, DT, N], F32R) for s in ("hi", "lo"))
        hid = sb("hid", [P, F])
        hT = hid[:, :].rearrange("p (k n) -> p k n", k=DT)
        s_hi, s_lo = (sb(f"s_{s}", [P, FT, P], F32R) for s in ("hi", "lo"))
        aside = sb("aside", [P, N])
        diag = aside[:, :].rearrange("p (n d) -> p n d", n=NT)
        mask_sb = sb("mask_sb", [P, NT])
        x2 = sb("x2", [P, NT, D])
        x_out = sb("x_out", [P, NT, D])
        adj_sb = sb("adj_sb", [P, NT, N])
        unlinked = sb("unlinked", [P, NT, N], BF16)
        hb = sb("hb", [P, NT, D])
        bT = sb("bT", [P, DT, N])
        qk = sb("qk", [P, 4, N], F32R)
        qk_stack = sb("qk_stack", [P, 4, 2, N], F32R)
        vals = sb("vals", [P, NT, D])
        prob = sb("prob", [P, 8, N])
        adjT_b = prob[:, 0:NT, :]
        pT = sb("pT", [P, HG, NT, N])
        region = pT[:, :, :, :].rearrange("p h j n -> p (h j n)")
        att = region[:, 0:2048].rearrange("p (m n) -> p m n", m=NT)
        sig = region[:, 2048:3072].rearrange("p (b n) -> p b n", b=2)
        lin = region[:, 3072:3072 + NT * DE].rearrange("p (n d) -> p n d", n=NT)
        msg = region[:, 5120:6144].rearrange("p (n d) -> p n d", n=NT)
        inv_x = sb("inv_x", [P, NT, HG, HD])
        small = sb("small", [P, 232])

        def norm_tiles(o):
            return (small[:, o:o + 24].rearrange("p (n k) -> p n k", n=NT),
                    small[:, o + 24:o + 32].rearrange("p (n k) -> p n k", n=NT),
                    *(small[:, o + 32 + 4 * i:o + 36 + 4 * i] for i in range(4)), small[:, o + 48:o + 49])

        ss = small[:, 100:108].rearrange("p (n c) -> p n c", n=NT)
        sse, rms, s2 = small[:, 108:112], small[:, 112:116], small[:, 116:120]
        den, rec, fac, rsum = (small[:, 120 + 4 * i:124 + 4 * i] for i in range(4))
        nmax = small[:, 136:168].rearrange("p (h n) -> p h n", h=H)
        prsum = small[:, 168:200].rearrange("p (h n) -> p h n", h=H)
        pinv = small[:, 200:216].rearrange("p (h n) -> p h n", h=HG)
        deg, dege, dinv = small[:, 216:220], small[:, 220:224], small[:, 224:228]

        FB = [ctx.enter_context(nc.psum_tensor(f"front{i}", [P, N], F32)) for i in range(3)]
        SB_ = [ctx.enter_context(nc.psum_tensor(f"score{i}", [P, N], F32)) for i in range(2)]
        TB = [ctx.enter_context(nc.psum_tensor(f"turn{i}", [P, N], F32)) for i in range(2)]
        VB = ctx.enter_context(nc.psum_tensor("value", [P, N], F32))

        waited = sem("waited")
        w_loaded, setup_dve, setup_act, setup_pool, setup_pe = (
            sem(n) for n in ("w_loaded", "setup_dve", "setup_act", "setup_pool", "setup_pe"))
        x_loaded, adj_loaded, adjT_f_loaded, adjT_b_loaded, mask_loaded, out_stored = (
            sem(n) for n in ("x_loaded", "adj_loaded", "adjT_f_loaded", "adjT_b_loaded", "mask_loaded", "out_stored"))
        stacked = [sem(f"stacked{i}") for i in range(4)]
        f_norm, b_norm = ({n: sem(f"{half}_{n}") for n in ("stats", "fenced", "means", "step", "normed", "ready")}
                          for half in ("front", "back"))
        diag_saved, diag_eps, diag_back = sem("diag_saved"), sem("diag_eps"), sem("diag_back")
        b2_added = sem("b2_added")
        agg_ps, T_hi_ready, T_lo_ready = sem("agg_ps"), sem("T_hi_ready"), sem("T_lo_ready")
        hid_ps, squared = sem("hid_ps"), sem("squared")
        rms_sum, rms_eps, rms_ready = sem("rms_sum"), sem("rms_eps"), sem("rms_ready")
        hid_ready, tanh_done, silu_ready = sem("hid_ready"), sem("tanh_done"), sem("silu_ready")
        f_turned = sem("f_turned")
        s_hi_ready, s_lo_ready = sem("s_hi_ready"), sem("s_lo_ready")
        down_ps, x0_ready = sem("down_ps"), sem("x0_ready")
        hT_act, hT_dve = sem("hT_act"), sem("hT_dve")
        lin_ps, s1_ps = sem("lin_ps"), sem("s1_ps")
        lin_act, lin_dve, s2_ready, ones_ready = (sem(n) for n in ("lin_act", "lin_dve", "s2_ready", "ones_ready"))
        sig_ready, att_ready, att_ps = sem("sig_ready"), sem("att_ready"), sem("att_ps")
        upd_step, x1_ready = sem("upd_step"), sem("x1_ready")
        table_in = sem("table_in")
        unlinked_ready, deg_ready = sem("unlinked_ready"), sem("deg_ready")
        deg_eps, dinv_ready, b3_added = sem("deg_eps"), sem("dinv_ready"), sem("b3_added")
        b_turned, N_turned = sem("b_turned"), 2 + 32 + 2 + 2
        bT_act, bT_dve = sem("bT_act"), sem("bT_dve")
        qk_ps, qk_hi_ready, qk_lo_ready = sem("qk_ps"), sem("qk_hi_ready"), sem("qk_lo_ready")
        v_ps, v_ready = sem("v_ps"), sem("v_ready")
        sc_ps, biased, exped = sem("sc_ps"), sem("biased"), sem("exped")
        pT_act, pT_dve = sem("pT_act"), sem("pT_dve")
        av_ps, inv_ready, invx_ready = sem("av_ps"), sem("inv_ready"), sem("invx_ready")
        lb_ready, o_ready = sem("lb_ready"), sem("o_ready")
        o_ps, x2_ready = sem("o_ps"), sem("x2_ready")
        sup_ps, sup_ready = sem("sup_ps"), sem("sup_ready")
        agg3_ps, out_ready = sem("agg3_ps"), sem("out_ready")

        freed = [(bT_act, 2, 1), (bT_dve, 2, 1)]
        n_act = n_dve = 0
        turn_of_prob, turn_of_inv = {}, {}
        DVE_TURN = 1
        for h in range(H):
            for j in range(NT):
                turn_of_prob[h, j] = len(freed)
                if j != DVE_TURN:
                    n_act += 1
                    freed.append((pT_act, 24, n_act))
                else:
                    n_dve += 1
                    freed.append((pT_dve, 8, n_dve))
            if h in (HG, H - 1):
                g = 0 if h == HG else 1
                turn_of_inv[g] = len(freed)
                freed.append((lb_ready, 2, g + 1))
        turn_of_L3 = len(freed)
        freed += [(bT_act, 2, 2), (bT_dve, 2, 2)]
        assert len(freed) == N_turned and N_turned % 2 == 0

        SETUP_DVE = 36

        def tile_steps(g):
            return [(n, g + 4 - 8 * n) for n in range(NT) if 0 <= g + 4 - 8 * n < 16]

        def quarters(n, u):
            if n == NT - 1:
                return range(4) if u == 8 else ()
            return (u - 11,) if 11 <= u < 15 else ()

        GRID = range(-4, 4 * H)
        Q1_STEP, K1_STEP = 0, 3

        def diag_of(tile):
            return bass.AP(tensor=tile, offset=0, ap=[[NT * N, P], [N + P, NT], [1, P]])

        def unregistered(eng):
            eng.sem_inc(waited)

        block = ctx.enter_context(nc.Block())

        @block.sync
        def _(sp):
            kp = "(k p) n -> p k n"
            sp.dma_start(region[:, 0:2048].rearrange("p (k n) -> p k n", k=DT), W1.rearrange(kp, p=P)).then_inc(w_loaded, 16)
            sp.dma_start(region[:, 2048:4096].rearrange("p (k n) -> p k n", k=FT), W2.rearrange(kp, p=P)).then_inc(w_loaded, 16)
            for i, w in enumerate((WqT, WkT, WvT, WoT, W3)):
                sp.dma_start(ws[:, i, :, :], w.rearrange(kp, p=P)).then_inc(w_loaded, 16)
            sp.dma_start(wl[:, :, 0:D], WL.rearrange(kp, p=P)).then_inc(w_loaded, 16)
            sp.dma_start(region[:, 7168:7680].rearrange("p (k n) -> p k n", k=DT), WLn.rearrange(kp, p=P)).then_inc(w_loaded, 16)
            for r in (0, 32):
                sp.dma_start(region[r:r + 1, 4096:4096 + F], b1[None, :]).then_inc(w_loaded, 16)
            sp.dma_start(rmsw_b[:, :], rmsw[None, :].to_broadcast([P, F])).then_inc(w_loaded, 16)
            for d, s in ((bL_b, bL), (b2_b, b2), (b3_b, b3)):
                sp.dma_start(d[:, :], s[None, :].to_broadcast([P, D])).then_inc(w_loaded, 16)
            sp.dma_start(cst[:, :], cols).then_inc(w_loaded, 16)

            rows = "o (n p) d -> p (o n) d"

            def load_x(b):
                sp.dma_start(x_in[:, :, :], x[bass.ds(b, 1)].rearrange(rows, p=P)).then_inc(x_loaded, 16)

            def load_mask(b):
                sp.dma_start(mask_sb[:, :], maskT[bass.ds(b, 1)].rearrange("o p n -> p (o n)")).then_inc(mask_loaded, 16)

            def load_adj(b):
                sp.dma_start(adj_sb[:, :, :], adj[bass.ds(b, 1)].rearrange(rows, p=P)).then_inc(adj_loaded, 16)

            def load_adjT_f(b):
                sp.dma_start(adjT_f[:, :, :], adjT[bass.ds(b, 1)].rearrange(rows, p=P)).then_inc(adjT_f_loaded, 16)

            def stack(t, h):
                g, s, r = h // HG, h % 4, slice(HD * (h % HG), HD * (h % HG) + HD)
                if h >= 4:
                    sp.wait_ge(sc_ps, at(t, 32, 4 * (h - 4) + 4))
                    unregistered(sp)
                elif later(t):
                    sp.wait_ge(sc_ps, at(t, 32, 0))
                    unregistered(sp)
                if h % HG == 0:
                    sp.wait_ge(qk_hi_ready, at(t, 4, 2 * g + 2))
                    unregistered(sp)
                    sp.wait_ge(qk_lo_ready, at(t, 4, 2 * g + 2))
                    unregistered(sp)
                for c, (q, k) in enumerate(((0, 2), (0, 3), (1, 2), (1, 3))):
                    sp.dma_start(qk_stack[HD * c:HD * c + HD, s, :, :].bitcast(F32),
                                 qk[r, q:k + 1:k - q, :].bitcast(F32)).then_inc(stacked[s], 16)

            def back2(t):
                for h in range(H):
                    stack(t, h)

            def phase_b(t, tf, follows, next_adj):
                if t is not None:
                    sp.wait_ge(b_turned, at(t, N_turned, turn_of_prob[H - 1, NT - 1] + 1))
                    unregistered(sp)
                    sp.dma_start(adjT_b, adjT[bass.ds(t, 1)].rearrange(rows, p=P)).then_inc(adjT_b_loaded, 16)
                    if next_adj:
                        load_adj(t + 1)
                if follows:
                    sp.wait_ge(att_ready, at(tf, 4, 4))
                    unregistered(sp)
                    load_adjT_f(tf + 1)
                    sp.wait_ge(x1_ready, at(tf, 4, 4))
                    unregistered(sp)
                    load_x(tf + 1)
                    load_mask(tf + 1)
                if t is not None:
                    sp.wait_ge(out_ready, at(t, 4, 4))
                    unregistered(sp)
                    sp.dma_start(out[bass.ds(t, 1)].rearrange(rows, p=P), x_out[:, :, :]).then_inc(out_stored, 16)

            load_x(0)
            load_adjT_f(0)
            load_mask(0)
            load_adj(0)
            phase_b(None, 0, True, False)
            back2(0)
            phase_b(0, 1, True, True)
            with sp.Fori(1, B - 2) as t:
                back2(t)
                phase_b(t, t + 1, True, True)
            back2(B - 2)
            phase_b(B - 2, B - 1, False, True)
            back2(B - 1)
            phase_b(B - 1, None, False, False)
            sp.wait_ge(out_stored, 16 * B)

        N_W = 16 * 16

        @block.gpsimd
        def _(pool):
            step = [0]

            def done(ins):
                step[0] += 1
                ins.then_inc(setup_pool, 1)
                pool.wait_ge(setup_pool, step[0])

            done(pool.memset(ident[:, :], 0.0))
            done(pool.affine_select(out=ident[:, :], in_=ident[:, :], compare_op=ALU.not_equal, fill=1.0,
                                    base=0, pattern=[[-1, P]], channel_multiplier=1))
            for c, v in ((k_rms, F * RMS_EPS), (k_ln, LN_EPS), (k_mhalf, -0.5), (k_deg, DEG_EPS), (k_neg1, -1.0)):
                done(pool.memset(c, v))
            pool.wait_ge(setup_dve, SETUP_DVE)

            def wide(c, n):
                return c.to_broadcast([P, n])

            def layernorm(t, l, norm, tiles):
                bn, mv, ve, rstd, nmean, nb, _ = tiles
                pool.wait_ge(norm["means"], at(t, 8, 4 * l + 4))
                if l or later(t):
                    pool.wait_ge(norm["ready"], at(t, 8, 4 * l))
                pool.tensor_tensor(ve, mv[:, :, 1], wide(k_ln, NT), ALU.add).then_inc(norm["step"], 1)
                pool.wait_ge(norm["step"], at(t, 6, 3 * l + 1))
                pool.tensor_tensor(rstd, ve, wide(k_mhalf, NT), ALU.pow).then_inc(norm["step"], 1)
                pool.wait_ge(norm["step"], at(t, 6, 3 * l + 2))
                pool.tensor_tensor(nmean, mv[:, :, 0], wide(k_neg1, NT), ALU.mult).then_inc(norm["step"], 1)
                pool.wait_ge(norm["step"], at(t, 6, 3 * l + 3))
                pool.tensor_tensor(nb, nmean, rstd, ALU.mult).then_inc(norm["normed"], 1)

            def add_b2(tf):
                pool.wait_ge(f_norm["ready"], at(tf, 8, 4))
                for n in range(NT):
                    ins = pool.tensor_tensor(x_in[:, n, :], x_in[:, n, :], b2_b[:, :], ALU.add)
                ins.then_inc(b2_added, 1)

            def hidden_norm(tf, n):
                pool.wait_ge(squared, at(tf, 8, 2 * n + 2))
                if later(tf):
                    pool.wait_ge(hid_ready, at(tf, 8, 0))
                pool.tensor_tensor(sse[:, n:n + 1], ss[:, n, 0:1], ss[:, n, 1:2], ALU.add).then_inc(rms_sum, 1)
                pool.wait_ge(rms_sum, at(tf, 4, n + 1))
                pool.tensor_tensor(sse[:, n:n + 1], sse[:, n:n + 1], k_rms, ALU.add).then_inc(rms_eps, 1)
                pool.wait_ge(rms_eps, at(tf, 4, n + 1))
                pool.tensor_tensor(rms[:, n:n + 1], sse[:, n:n + 1], k_mhalf, ALU.pow).then_inc(rms_ready, 1)

            def degrees(t):
                pool.wait_ge(deg_ready, at(t, 1, 1))
                pool.tensor_tensor(dege, deg, wide(k_deg, NT), ALU.add).then_inc(deg_eps, 1)
                pool.wait_ge(deg_eps, at(t, 1, 1))
                pool.tensor_tensor(dinv, dege, wide(k_mhalf, NT), ALU.pow).then_inc(dinv_ready, 1)

            def widen_inverse(t, g):
                pool.wait_ge(inv_ready, at(t, 2, g + 1))
                if g == 1:
                    pool.wait_ge(b_turned, at(t, N_turned, turn_of_inv[0] + 1))
                for n in range(NT):
                    ins = pool.tensor_tensor(inv_x[:, n, :, :], pinv[:, :, n].unsqueeze(2).to_broadcast([P, HG, HD]),
                                             one_b.unsqueeze(2).to_broadcast([P, HG, HD]), ALU.mult)
                ins.then_inc(invx_ready, 1)

            def add_b3(t):
                pool.wait_ge(x2_ready, at(t, 4, 4))
                if later(t):
                    pool.wait_ge(out_stored, t * 16)
                for n in range(NT):
                    ins = pool.tensor_tensor(x_out[:, n, :], x2[:, n, :], b3_b[:, :], ALU.add)
                ins.then_inc(b3_added, 1)

            def phases(t, tf):
                if tf is not None:
                    layernorm(tf, 0, f_norm, norm_tiles(0))
                    add_b2(tf)
                if t is not None:
                    degrees(t)
                if tf is not None:
                    hidden_norm(tf, 0)
                    hidden_norm(tf, 1)
                if t is not None:
                    widen_inverse(t, 0)
                if tf is not None:
                    hidden_norm(tf, 2)
                    hidden_norm(tf, 3)
                if t is not None:
                    widen_inverse(t, 1)
                if tf is not None:
                    layernorm(tf, 1, f_norm, norm_tiles(0))
                if t is not None:
                    layernorm(t, 1, b_norm, norm_tiles(50))
                    add_b3(t)
                if tf is not None:
                    layernorm(tf, 0, b_norm, norm_tiles(50))

            phases(None, 0)
            phases(0, 1)
            with pool.Fori(1, B - 1) as t:
                phases(t, t + 1)
            phases(B - 1, None)

        @block.scalar
        def _(act):
            act.wait_ge(w_loaded, N_W)

            def hi(dst, src):
                return act.activation(dst, src, ACT.Identity)

            hi(w1_hi[:, :, :], region[:, 0:2048].rearrange("p (k n) -> p k n", k=DT)).then_inc(setup_act, 1)
            hi(w2_hi[:, :, :], region[:, 2048:4096].rearrange("p (k n) -> p k n", k=FT)).then_inc(setup_act, 1)
            act.wait_ge(setup_dve, SETUP_DVE)

            def layernorm(t, l, norm, tiles, src, dst):
                bn, mv, ve, rstd, nmean, nb, _ = tiles
                act.wait_ge(norm["normed"], at(t, 2, l + 1))
                for n in range(NT):
                    act.activation(dst[:, n, :], src[:, n, :], ACT.Relu, bias=nb[:, n:n + 1],
                                   scale=rstd[:, n:n + 1]).then_inc(norm["ready"], 1)

            def load_table(tf, k, function):
                if k > 1 or later(tf):
                    act.wait_ge(table_in, at(tf, 2, k - 1))
                act.activation(small[:, 230:231], k_ln, function).then_inc(table_in, 1)

            def norm0(tf):
                if later(tf):
                    act.wait_ge(f_turned, at(tf, 10, 0))
                layernorm(tf, 0, f_norm, norm_tiles(0), x_in, hf)

            def aggregated(tf):
                for d in range(DT):
                    act.wait_ge(agg_ps, at(tf, 2, d + 1))
                    hi(T_hi[:, d, :], FB[d][:, :]).then_inc(T_hi_ready, 1)

            def square(tf, n, c):
                act.wait_ge(hid_ps, at(tf, 8, 2 * n + c + 1))
                if n == 0 and c == 0:
                    act.wait_ge(diag_back, at(tf, 1, 1))
                    if later(tf):
                        act.wait_ge(rms_ready, at(tf, 4, 0))
                elif c == 0:
                    act.wait_ge(silu_ready, at(tf, 8, 2 * n))
                else:
                    act.wait_ge(squared, at(tf, 8, 2 * n + 1))
                act.activation(aside[:, :], FB[c][:, :], ACT.Square, accum_out=ss[:, n, c:c + 1]).then_inc(squared, 1)

            def tanh(tf, n, c):
                act.wait_ge(hid_ready, at(tf, 8, 2 * n + c + 1))
                if c:
                    act.wait_ge(silu_ready, at(tf, 8, 2 * n + 1))
                act.activation(aside[:, :], hid[:, N * c:N * c + N], ACT.Tanh).then_inc(tanh_done, 1)

            def hidden_hi(tf, n, c):
                act.wait_ge(f_turned, at(tf, 10, 2 * n + c + 1))
                if n:
                    act.wait_ge(down_ps, at(tf, 16, 4 * n + 2 * c - 2))
                elif later(tf):
                    act.wait_ge(down_ps, at(tf, 16, 0))
                hi(s_hi[:, 4 * c:4 * c + 4, :].rearrange("p f n -> p (f n)"), FB[c][:, :]).then_inc(s_hi_ready, 1)

            def turned1(tf):
                act.wait_ge(f_turned, at(tf, 10, 9))
                act.activation(hT[:, 0, :], FB[0][:, :], ACT.Copy).then_inc(hT_act, 1)

            def linear(tf, n):
                if n == 0 and later(tf):
                    act.wait_ge(av_ps, at(tf, 8, 0))
                act.wait_ge(s2_ready, at(tf, 4, n + 1))
                act.activation(lin[:, n, 0:D], FB[0][:, 0:D], ACT.Copy).then_inc(lin_act, 1)

            def sigmoid(tf, m):
                if m == 0:
                    act.wait_ge(s1_ps, at(tf, 1, 1))
                act.wait_ge(s2_ready, at(tf, 4, m + 1))
                if m >= 2:
                    act.wait_ge(att_ready, at(tf, 4, m - 1))
                act.activation(sig[:, m % 2, :], FB[2][:, :], ACT.Sigmoid, bias=s2[:, m:m + 1]).then_inc(sig_ready, 1)

            def turned(t, i, first):
                act.wait_ge(b_turned, at(t, N_turned, first + 1))
                act.activation(bT[:, 0, :], TB[0][:, :], ACT.Copy).then_inc(bT_act, 1)

            def qk_high(t, g, i):
                act.wait_ge(qk_ps, at(t, 4, 2 * g + i + 1))
                if g == 1 and i == 0:
                    for s in range(4):
                        act.wait_ge(stacked[s], at(t, 128, 64))
                ps = VB if g else SB_[i]
                act.activation(qk[:, 2 * i, :], ps[:, :], ACT.Identity,
                               scale=1.0 if i else q_scale[:, g:g + 1]).then_inc(qk_hi_ready, 1)

            def values(t, j):
                act.wait_ge(v_ps, at(t, 2, j + 1))
                act.activation(vals[:, 2 * j:2 * j + 2, :].rearrange("p a d -> p (a d)"), VB[:, :], ACT.Copy).then_inc(v_ready, 1)

            def exps(t, i):
                h, n = divmod(i, NT)
                act.wait_ge(biased, at(t, 32, i + 1))
                act.activation(prob[:, i % 8, :], prob[:, i % 8, :], ACT.Exp, bias=nmax[:, h, n:n + 1],
                               scale=-1.0, accum_out=prsum[:, h, n:n + 1]).then_inc(exped, 1)

            def turned_probs(t, h, j):
                if h == HG:
                    act.wait_ge(av_ps, at(t, 8, j + 1))
                k = turn_of_prob[h, j]
                act.wait_ge(b_turned, at(t, N_turned, k + 1))
                act.activation(pT[:, h % HG, j, :], TB[k % 2][:, :], ACT.Copy).then_inc(pT_act, 1)

            def support(t, n):
                if n == 0:
                    act.wait_ge(dinv_ready, at(t, 1, 1))
                act.wait_ge(sup_ps, at(t, 4, n + 1))
                act.activation(vals[:, n, :], SB_[n % 2][:, 0:D], ACT.Copy, scale=dinv[:, n:n + 1]).then_inc(sup_ready, 1)

            def phases(t, tf):
                b, f = t is not None, tf is not None
                if b:
                    turned(t, 0, 0)
                if f:
                    norm0(tf)
                if b:
                    qk_high(t, 0, 0)
                    qk_high(t, 0, 1)
                    values(t, 0)
                if f:
                    aggregated(tf)
                if b:
                    values(t, 1)
                for g in GRID:
                    if f:
                        for n, u in tile_steps(g):
                            if u in (1, 2):
                                square(tf, n, u - 1)
                            elif u in (4, 5):
                                tanh(tf, n, u - 4)
                            elif u in (6, 7):
                                hidden_hi(tf, n, u - 6)
                    if b and g + 4 < 4 * H:
                        exps(t, g + 4)
                    if b and g >= 0 and g % 4 != DVE_TURN:
                        turned_probs(t, g // 4, g % 4)
                    if b and g == Q1_STEP + 1:
                        qk_high(t, 1, 0)
                    if b and g == K1_STEP + 1:
                        qk_high(t, 1, 1)
                if f:
                    layernorm(tf, 1, f_norm, norm_tiles(0), x_in, hf)
                    turned1(tf)
                    load_table(tf, 1, ACT.Sigmoid)
                    linear(tf, 0)
                if b:
                    layernorm(t, 1, b_norm, norm_tiles(50), x2, hb)
                if f:
                    linear(tf, 2)
                if b:
                    turned(t, 1, turn_of_L3)
                for n in range(NT):
                    if f:
                        sigmoid(tf, n)
                    if b:
                        support(t, n)
                if f:
                    load_table(tf, 2, ACT.Exp)
                    layernorm(tf, 0, b_norm, norm_tiles(50), x2, hb)

            phases(None, 0)
            phases(0, 1)
            with act.Fori(1, B - 1) as t:
                phases(t, t + 1)
            phases(B - 1, None)

        @block.vector
        def _(dve):
            step = [0]

            def done(ins):
                step[0] += 1
                ins.then_inc(setup_dve, 1)
                dve.wait_ge(setup_dve, step[0])

            def lo(dst, src, high):
                return dve.tensor_tensor(dst, src, high.bitcast(F32), ALU.subtract)

            for tile in (b1_rows, ones_rows):
                done(dve.memset(tile[:, :].bitcast(F32), 0.0))
            for r in (0, 32):
                done(dve.memset(ones_rows[r:r + 1, :].bitcast(F32), 1.0))
            done(dve.memset(one_b, 1.0))
            dve.wait_ge(w_loaded, N_W)
            b1_stage = region[:, 4096:4096 + F]
            for r in (0, 32):
                done(dve.tensor_copy(b1_rows[r:r + 1, :], b1_stage[r:r + 1, :]))
            done(lo(b1_rows[32:33, :], b1_stage[32:33, :], b1_rows[32:33, :]))
            done(dve.tensor_scalar(rmsw_b[:, :], rmsw_b[:, :], 0.5 * float(F) ** 0.5, None, ALU.mult))
            for w, sgn, mag in ((cst[:, 8:16], t8, t8b), (cst[:, 6:8], t2, t2b)):
                done(dve.tensor_scalar(sgn, w, 0.0, 2.0, ALU.is_ge, ALU.mult))
                done(dve.tensor_scalar(sgn, sgn, 1.0, None, ALU.subtract))
                done(dve.tensor_tensor(mag, w, sgn, ALU.mult))
                done(dve.tensor_scalar(mag, mag, TINY, None, ALU.max))
            done(dve.scalar_tensor_tensor(out=neg_w, in0=t8b, scalar=-1.0, in1=t8, op0=ALU.mult, op1=ALU.mult))
            done(dve.scalar_tensor_tensor(out=t2c, in0=t2b, scalar=HD ** 0.5, in1=t2, op0=ALU.mult, op1=ALU.mult))
            done(dve.reciprocal(q_scale, t2c))
            dve.wait_ge(setup_pool, 7)
            for h in range(H):
                done(dve.tensor_scalar(neg_mask[:, h, :], ident[:, :], t8[:, h:h + 1], -BIG, ALU.mult, ALU.mult))
            dve.wait_ge(setup_act, 2)
            done(lo(w1_lo[:, :, :], region[:, 0:2048].rearrange("p (k n) -> p k n", k=DT), w1_hi[:, :, :]))
            done(lo(w2_lo[:, :, :], region[:, 2048:4096].rearrange("p (k n) -> p k n", k=FT), w2_hi[:, :, :]))
            dve.wait_ge(setup_pe, 1)
            for k in range(DT):
                done(dve.tensor_copy(wl[:, k, D:DE], FB[k][:, 0:2]))
                done(dve.tensor_copy(wa[:, k, :], wl[:, k, D + 1:D + 2].to_broadcast([P, P])))
            done(dve.tensor_copy(t2, FB[2][:, 0:2]))
            done(dve.tensor_scalar(s_const, t2[:, 0:1], t2[:, 1:2], cst[:, 17:18], ALU.add, ALU.add))
            assert step[0] == SETUP_DVE, step[0]

            def stats(t, l, norm, tiles, src, n):
                if src is x_in and l == 1:
                    dve.wait_ge(x0_ready, at(t, 4, n + 1))
                elif src is x2:
                    dve.wait_ge(x2_ready if l else x1_ready, at(t, 4, n + 1))
                dve.bn_stats(tiles[0][:, n, :], src[:, n, :]).then_inc(norm["stats"], 1)

            def means(t, l, norm, tiles):
                bn, mv, ve, rstd, nmean, nb, fence = tiles
                if l or later(t):
                    dve.wait_ge(norm["normed"], at(t, 2, l))
                dve.wait_ge(norm["stats"], at(t, 8, 4 * l + 4))
                dve.memset(fence, 0.0).then_inc(norm["fenced"], 1)
                for n in range(NT):
                    dve.bn_aggr(mv[:, n, :], bn[:, n, :]).then_inc(norm["means"], 1)

            def stats0(tf):
                dve.wait_ge(x_loaded, at(tf, 16, 16))
                for n in range(NT):
                    stats(tf, 0, f_norm, norm_tiles(0), x_in, n)
                means(tf, 0, f_norm, norm_tiles(0))

            def diagonal(tf):
                dve.wait_ge(adjT_f_loaded, at(tf, 16, 16))
                if later(tf):
                    dve.wait_ge(silu_ready, at(tf, 8, 0))
                dve.tensor_copy(diag, diag_of(adjT_f)).then_inc(diag_saved, 1)
                dve.wait_ge(diag_saved, at(tf, 1, 1))
                dve.scalar_tensor_tensor(out=diag_of(adjT_f), in0=ident[:, :].unsqueeze(1).to_broadcast([P, NT, P]),
                                         scalar=cst[:, 16:17], in1=diag, op0=ALU.mult, op1=ALU.add).then_inc(diag_eps, 1)

            def aggregated(tf):
                for d in range(DT):
                    dve.wait_ge(T_hi_ready, at(tf, 2, d + 1))
                    lo(T_lo[:, d, :], FB[d][:, :], T_hi[:, d, :]).then_inc(T_lo_ready, 1)
                dve.wait_ge(diag_eps, at(tf, 1, 1))
                dve.tensor_copy(diag_of(adjT_f), diag).then_inc(diag_back, 1)

            def hidden(tf, n):
                dve.wait_ge(rms_ready, at(tf, 4, n + 1))
                if n:
                    dve.wait_ge(f_turned, at(tf, 10, 2 * n))
                for c in range(2):
                    cs = slice(N * c, N * c + N)
                    dve.scalar_tensor_tensor(out=hid[:, cs], in0=FB[c][:, :], scalar=rms[:, n:n + 1], in1=rmsw_b[:, cs],
                                             op0=ALU.mult, op1=ALU.mult).then_inc(hid_ready, 1)

            def silu(tf, n, c):
                cs = slice(N * c, N * c + N)
                dve.wait_ge(tanh_done, at(tf, 8, 2 * n + c + 1))
                dve.scalar_tensor_tensor(out=hid[:, cs], in0=aside[:, :], scalar=1.0, in1=hid[:, cs],
                                         op0=ALU.add, op1=ALU.mult).then_inc(silu_ready, 1)

            def hidden_lo(tf, n, c):
                dve.wait_ge(s_hi_ready, at(tf, 8, 2 * n + c + 1))
                f = slice(4 * c, 4 * c + 4)
                lo(s_lo[:, f, :].rearrange("p f n -> p (f n)"), FB[c][:, :],
                   s_hi[:, f, :].rearrange("p f n -> p (f n)")).then_inc(s_lo_ready, 1)

            def update0(tf, n):
                if n == 0:
                    dve.wait_ge(b2_added, at(tf, 1, 1))
                dve.wait_ge(down_ps, at(tf, 16, 4 * n + 4))
                dve.tensor_tensor(x_in[:, n, :], FB[2][:, 0:D], x_in[:, n, :], ALU.add).then_inc(x0_ready, 1)

            def turned1(tf):
                dve.wait_ge(f_turned, at(tf, 10, 10))
                dve.tensor_copy(hT[:, 1, :], FB[1][:, :]).then_inc(hT_dve, 1)

            def linear(tf):
                if later(tf):
                    dve.wait_ge(av_ps, at(tf, 8, 0))
                    dve.wait_ge(sig_ready, at(tf, 4, 0))
                for n in range(NT):
                    dve.wait_ge(lin_ps, at(tf, 4, n + 1))
                    if n % 2:
                        dve.tensor_copy(lin[:, n, 0:D], FB[1][:, 0:D]).then_inc(lin_dve, 1)
                    dve.tensor_scalar(s2[:, n:n + 1], FB[n % 2][:, D:D + 1], s_const, None, ALU.add).then_inc(s2_ready, 1)
                dve.memset(lin[:, :, D:DE], 1.0).then_inc(ones_ready, 1)

            def attention1(tf):
                dve.wait_ge(mask_loaded, at(tf, 16, 16))
                for m in range(NT):
                    dve.wait_ge(sig_ready, at(tf, 4, m + 1))
                    dve.scalar_tensor_tensor(out=att[:, m, :], in0=sig[:, m % 2, :], scalar=mask_sb[:, m:m + 1],
                                             in1=adjT_f[:, m, :], op0=ALU.mult, op1=ALU.mult).then_inc(att_ready, 1)

            def update1(tf):
                if later(tf):
                    dve.wait_ge(b_norm["ready"], at(tf, 8, 0))
                    dve.wait_ge(b3_added, at(tf, 1, 0))
                for n in range(NT):
                    c = slice(n, n + 1)
                    ps = FB[n % 2]
                    dve.wait_ge(att_ps, at(tf, 4, n + 1))
                    dve.tensor_copy(rsum[:, c], ps[:, D:D + 1]).then_inc(upd_step, 1)
                    dve.tensor_scalar(den[:, c], ps[:, D:D + 1], mask_sb[:, c], ATT_EPS, ALU.mult, ALU.add).then_inc(upd_step, 1)
                    dve.wait_ge(upd_step, at(tf, 20, 5 * n + 2))
                    dve.scalar_tensor_tensor(out=msg[:, n, :], in0=bL_b[:, :], scalar=rsum[:, c], in1=ps[:, 0:D],
                                             op0=ALU.mult, op1=ALU.add).then_inc(upd_step, 1)
                    dve.reciprocal(rec[:, c], den[:, c]).then_inc(upd_step, 1)
                    dve.wait_ge(upd_step, at(tf, 20, 5 * n + 4))
                    dve.tensor_scalar(fac[:, c], rec[:, c], mask_sb[:, c], mask_sb[:, c], ALU.mult, ALU.mult).then_inc(upd_step, 1)
                    dve.wait_ge(upd_step, at(tf, 20, 5 * n + 5))
                    dve.scalar_tensor_tensor(out=x2[:, n, :], in0=msg[:, n, :], scalar=fac[:, c], in1=x_in[:, n, :],
                                             op0=ALU.mult, op1=ALU.add).then_inc(x1_ready, 1)
                    if n:
                        stats(tf, 0, b_norm, norm_tiles(50), x2, n - 1)
                stats(tf, 0, b_norm, norm_tiles(50), x2, NT - 1)

            def graph(t):
                dve.wait_ge(adj_loaded, at(t, 16, 16))
                if later(t):
                    dve.wait_ge(sc_ps, at(t, 32, 0))
                    dve.wait_ge(dinv_ready, at(t, 1, 0))
                dve.tensor_scalar(unlinked[:, :, :], adj_sb[:, :, :], 0.0, None, ALU.is_equal).then_inc(unlinked_ready, 1)
                dve.tensor_reduce(deg, adj_sb[:, :, :], AX.X, ALU.add).then_inc(deg_ready, 1)

            def turned(t, i, first):
                dve.wait_ge(b_turned, at(t, N_turned, first + 2))
                dve.tensor_copy(bT[:, 1, :], TB[1][:, :]).then_inc(bT_dve, 1)

            def qk_low(t, g, i):
                dve.wait_ge(qk_hi_ready, at(t, 4, 2 * g + i + 1))
                if i == 0:
                    dve.scalar_tensor_tensor(out=qk[:, 1, :], in0=(VB if g else SB_[0])[:, :], scalar=q_scale[:, g:g + 1],
                                             in1=qk[:, 0, :].bitcast(F32), op0=ALU.mult,
                                             op1=ALU.subtract).then_inc(qk_lo_ready, 1)
                else:
                    lo(qk[:, 3, :], (VB if g else SB_[1])[:, :], qk[:, 2, :]).then_inc(qk_lo_ready, 1)

            def bias(t, i):
                h, n = divmod(i, NT)
                dve.wait_ge(sc_ps, at(t, 32, i + 1))
                if n == 0 and h >= 2:
                    dve.wait_ge(b_turned, at(t, N_turned, turn_of_prob[h - 2, NT - 1] + 1))
                unregistered(dve)
                dve.tensor_tensor_reduce(out=prob[:, i % 8, :], in0=SB_[i % 2][:, :], in1=adj_sb[:, n, :],
                                         scale=neg_w[:, h:h + 1], scalar=3e38, op0=ALU.add, op1=ALU.min,
                                         accum_out=nmax[:, h, n:n + 1]).then_inc(biased, 1)

            def turned_probs(t, h):
                if h == HG:
                    dve.wait_ge(av_ps, at(t, 8, DVE_TURN + 1))
                k = turn_of_prob[h, DVE_TURN]
                dve.wait_ge(b_turned, at(t, N_turned, k + 1))
                dve.tensor_copy(pT[:, h % HG, DVE_TURN, :], TB[k % 2][:, :]).then_inc(pT_dve, 1)

            def inverse(t, g):
                dve.wait_ge(exped, at(t, 32, 16 * g + 16))
                if g or later(t):
                    dve.wait_ge(invx_ready, at(t, 2, g))
                dve.reciprocal(pinv[:, :, :].rearrange("p h n -> p (h n)"),
                               prsum[:, HG * g:HG * g + HG, :].rearrange("p h n -> p (h n)")).then_inc(inv_ready, 1)

            def attended(t, g):
                k = turn_of_inv[g]
                dve.wait_ge(b_turned, at(t, N_turned, k + 1))
                dve.tensor_copy(bT[:, g, :], TB[k % 2][:, :]).then_inc(lb_ready, 1)
                dve.wait_ge(lb_ready, at(t, 2, g + 1))
                dve.wait_ge(av_ps, at(t, 8, 4 * g + 4))
                dve.tensor_tensor(bT[:, g, :], VB[:, :], bT[:, g, :], ALU.mult).then_inc(o_ready, 1)

            def update2(t):
                for n in range(NT):
                    dve.wait_ge(o_ps, at(t, 4, n + 1))
                    dve.tensor_tensor(x2[:, n, :], SB_[n % 2][:, 0:D], x2[:, n, :], ALU.add).then_inc(x2_ready, 1)
                    if n:
                        stats(t, 1, b_norm, norm_tiles(50), x2, n - 1)
                stats(t, 1, b_norm, norm_tiles(50), x2, NT - 1)

            def update3(t):
                dve.wait_ge(b3_added, at(t, 1, 1))
                dve.wait_ge(dinv_ready, at(t, 1, 1))
                for n in range(NT):
                    dve.wait_ge(agg3_ps, at(t, 4, n + 1))
                    dve.scalar_tensor_tensor(out=x_out[:, n, :], in0=SB_[n % 2][:, 0:D], scalar=dinv[:, n:n + 1],
                                             in1=x_out[:, n, :], op0=ALU.mult, op1=ALU.add).then_inc(out_ready, 1)

            def phases(t, tf):
                b, f = t is not None, tf is not None
                if b:
                    turned(t, 0, 0)
                if f:
                    stats0(tf)
                    diagonal(tf)
                if b:
                    qk_low(t, 0, 0)
                    qk_low(t, 0, 1)
                    graph(t)
                if f:
                    aggregated(tf)
                for g in GRID:
                    if b and g + 4 < 4 * H:
                        bias(t, g + 4)
                    if f:
                        for n, u in tile_steps(g):
                            if u == 3:
                                hidden(tf, n)
                            elif u in (4, 5):
                                silu(tf, n, u - 4)
                            elif u in (6, 7):
                                hidden_lo(tf, n, u - 6)
                            elif u == (9 if n == NT - 1 else 15):
                                update0(tf, n)
                                stats(tf, 1, f_norm, norm_tiles(0), x_in, n)
                    if b and g >= 0 and g % 4 == DVE_TURN:
                        turned_probs(t, g // 4)
                    if b and g == Q1_STEP + 1:
                        qk_low(t, 1, 0)
                    if b and g == K1_STEP + 1:
                        qk_low(t, 1, 1)
                    if b and g == 4 * HG - 2:
                        inverse(t, 0)
                    if b and g == 4 * H - 4:
                        inverse(t, 1)
                    if b and g == 4 * HG + 4:
                        attended(t, 0)
                if f:
                    means(tf, 1, f_norm, norm_tiles(0))
                if b:
                    attended(t, 1)
                if f:
                    turned1(tf)
                if b:
                    update2(t)
                    means(t, 1, b_norm, norm_tiles(50))
                if f:
                    linear(tf)
                if b:
                    turned(t, 1, turn_of_L3)
                if f:
                    attention1(tf)
                    update1(tf)
                    means(tf, 0, b_norm, norm_tiles(50))
                if b:
                    update3(t)

            phases(None, 0)
            phases(0, 1)
            with dve.Fori(1, B - 1) as t:
                phases(t, t + 1)
            phases(B - 1, None)

        @block.tensor
        def _(pe):
            def product(ps, a, b, start, stop):
                pe.matmul(ps, a[0], b[0], start=start, stop=False)
                pe.matmul(ps, a[0], b[1], start=False, stop=False)
                return pe.matmul(ps, a[1], b[0], start=False, stop=stop)

            def tile(n):
                return slice(P * n, P * n + P)

            pe.wait_ge(w_loaded, N_W)
            wln = region[:, 7168:7680].rearrange("p (k n) -> p k n", k=DT)
            for i in range(DT):
                for k in range(DT):
                    pe.matmul(FB[i][:, 0:2], wln[:, k, tile(i)], cst[:, 2 * k:2 * k + 2], start=(k == 0), stop=(k == DT - 1))
            for k in range(DT):
                last = pe.matmul(FB[2][:, 0:2], cst[:, 4 + k:5 + k].to_broadcast([P, P]), cst[:, 2 * k:2 * k + 2],
                                 start=(k == 0), stop=(k == DT - 1))
            last.then_inc(setup_pe, 1)
            pe.wait_ge(setup_dve, SETUP_DVE)

            def aggregate(tf):
                pe.wait_ge(f_norm["ready"], at(tf, 8, 4))
                pe.wait_ge(diag_eps, at(tf, 1, 1))
                if later(tf):
                    pe.wait_ge(x1_ready, at(tf, 4, 0))
                for d in range(DT):
                    for m in range(NT):
                        last = pe.matmul(FB[d][:, :], hf[:, m, tile(d)], adjT_f[:, m, :], start=(m == 0), stop=(m == NT - 1))
                    last.then_inc(agg_ps, 1)

            def hidden(tf, n, c):
                if n:
                    pe.wait_ge(s_hi_ready, at(tf, 8, 2 * n + c - 1))
                    pe.wait_ge(s_lo_ready, at(tf, 8, 2 * n + c - 1))
                cs = slice(N * c, N * c + N)
                if n == 0:
                    pe.wait_ge(T_lo_ready, at(tf, 2, c + 1))
                pe.matmul(FB[c][:, :], ones_rows[:, :], b1_rows[:, cs], start=True, stop=False)
                for k in range(DT):
                    if n == 0 and c == 0 and k:
                        pe.wait_ge(T_lo_ready, at(tf, 2, k + 1))
                    last = product(FB[c][:, :], (T_hi[:, k, tile(n)], T_lo[:, k, tile(n)]),
                                   (w1_hi[:, k, cs], w1_lo[:, k, cs]), False, k == DT - 1)
                last.then_inc(hid_ps, 1)

            def turn_hidden(tf, n, c):
                pe.wait_ge(silu_ready, at(tf, 8, 2 * n + c + 1))
                for f in range(4):
                    last = pe.transpose(FB[c][:, tile(f)], hid[:, tile(4 * c + f)], ident[:, :])
                last.then_inc(f_turned, 1)

            def down(tf, n, q):
                c = q // 2
                pe.wait_ge(s_hi_ready, at(tf, 8, 2 * n + c + 1))
                pe.wait_ge(s_lo_ready, at(tf, 8, 2 * n + c + 1))
                if q == 0 and n:
                    pe.wait_ge(x0_ready, at(tf, 4, n))
                elif q == 0 and later(tf):
                    pe.wait_ge(sig_ready, at(tf, 4, 0))
                for f in range(2 * q, 2 * q + 2):
                    last = product(FB[2][:, 0:D], (s_hi[:, f, :], s_lo[:, f, :]), (w2_hi[:, f, :], w2_lo[:, f, :]),
                                   f == 0, f == FT - 1)
                last.then_inc(down_ps, 1)

            def turn1(tf):
                for n in range(NT):
                    pe.wait_ge(f_norm["ready"], at(tf, 8, n + 5))
                    for d in range(DT):
                        ins = pe.transpose(FB[d][:, tile(n)], hf[:, n, tile(d)], ident[:, :])
                        if n == NT - 1:
                            ins.then_inc(f_turned, 1)

            def linear(tf):
                pe.wait_ge(x0_ready, at(tf, 4, 4))
                pe.wait_ge(hT_act, at(tf, 1, 1))
                pe.wait_ge(hT_dve, at(tf, 1, 1))
                for k in range(DT):
                    last = pe.matmul(FB[2][:, :], wa[:, k, :], hT[:, k, :], start=(k == 0), stop=(k == DT - 1))
                last.then_inc(s1_ps, 1)
                for n in range(NT):
                    if n >= 2:
                        pe.wait_ge(s2_ready, at(tf, 4, n - 1))
                    if n == 2:
                        pe.wait_ge(lin_act, at(tf, 2, 1))
                    if n == 3:
                        pe.wait_ge(lin_dve, at(tf, 2, 1))
                    for k in range(DT):
                        last = pe.matmul(FB[n % 2][:, 0:DE], hT[:, k, tile(n)], wl[:, k, :], start=(k == 0), stop=(k == DT - 1))
                    last.then_inc(lin_ps, 1)

            def attend1(tf):
                pe.wait_ge(lin_act, at(tf, 2, 2))
                pe.wait_ge(lin_dve, at(tf, 2, 2))
                pe.wait_ge(s2_ready, at(tf, 4, 4))
                pe.wait_ge(ones_ready, at(tf, 1, 1))
                for n in range(NT):
                    if n >= 2:
                        pe.wait_ge(x1_ready, at(tf, 4, n - 1))
                    for m in range(NT):
                        if n == 0:
                            pe.wait_ge(att_ready, at(tf, 4, m + 1))
                        last = pe.matmul(FB[n % 2][:, 0:DE], att[:, m, tile(n)], lin[:, m, :], start=(m == 0), stop=(m == NT - 1))
                    last.then_inc(att_ps, 1)

            def wait_bank(t, k):
                if k >= 2:
                    s, per, n = freed[k - 2]
                    pe.wait_ge(s, at(t, per, n))
                elif later(t):
                    s, per, n = freed[N_turned - 2 + k]
                    pe.wait_ge(s, at(t, per, 0))

            def turn(t, l, first):
                for d in range(DT):
                    wait_bank(t, first + d)
                for n in range(NT):
                    pe.wait_ge(b_norm["ready"], at(t, 8, 4 * l + n + 1))
                    for d in range(DT):
                        ins = pe.transpose(TB[(first + d) % 2][:, tile(n)], hb[:, n, tile(d)], ident[:, :])
                        if n == NT - 1:
                            ins.then_inc(b_turned, 1)

            def project_qk(t, g, i):
                if g == 1:
                    if i == 0:
                        pe.wait_ge(v_ready, at(t, 2, 2))
                    else:
                        pe.wait_ge(qk_lo_ready, at(t, 4, 3))
                elif i == 0:
                    pe.wait_ge(bT_act, at(t, 2, 1))
                    pe.wait_ge(bT_dve, at(t, 2, 1))
                    if later(t):
                        pe.wait_ge(out_ready, at(t, 4, 0))
                for k in range(DT):
                    last = pe.matmul((VB if g else SB_[i])[:, :], ws[:, (WQ, WK)[i], k, tile(g)], bT[:, k, :],
                                     start=(k == 0), stop=(k == DT - 1))
                last.then_inc(qk_ps, 1)

            def project_v(t, j):
                if j:
                    pe.wait_ge(v_ready, at(t, 2, 1))
                elif later(t):
                    pe.wait_ge(o_ready, at(t, 2, 0))
                for i in range(2):
                    for k in range(DT):
                        last = pe.matmul(VB[:, D * i:D * i + D], bT[:, k, tile(2 * j + i)], ws[:, WV, k, :],
                                         start=(k == 0), stop=(k == DT - 1))
                last.then_inc(v_ps, 1)

            def scores(t, i):
                h, n = divmod(i, NT)
                if n == 0:
                    pe.wait_ge(stacked[h % 4], at(t, 128, 64 * (h // 4 + 1)))
                if i == 0:
                    pe.wait_ge(unlinked_ready, at(t, 1, 1))
                    pe.wait_ge(qk_lo_ready, at(t, 4, 2))
                if i >= 2:
                    pe.wait_ge(biased, at(t, 32, i - 1))
                pe.matmul(SB_[i % 2][:, :], qk_stack[:, h % 4, 0, tile(n)], qk_stack[:, h % 4, 1, :], start=True, stop=False)
                pe.matmul(SB_[i % 2][:, :], neg_mask[:, h, :], unlinked[:, n, :],
                          start=False, stop=True).then_inc(sc_ps, 1)

            def turn_probs(t, h, j):
                if j == 0:
                    pe.wait_ge(exped, at(t, 32, 4 * h + 4))
                k = turn_of_prob[h, j]
                wait_bank(t, k)
                for n in range(NT):
                    last = pe.transpose(TB[k % 2][:, tile(n)], prob[:, (4 * h + n) % 8, tile(j)], ident[:, :])
                last.then_inc(b_turned, 1)

            def attend(t, g, j):
                if j != DVE_TURN:
                    pe.wait_ge(pT_act, at(t, 24, 12 * g + 10 + j - (j > DVE_TURN)))
                else:
                    pe.wait_ge(pT_dve, at(t, 8, 4 * g + 4))
                if j == 0:
                    if g == 0:
                        pe.wait_ge(qk_lo_ready, at(t, 4, 4))
                    else:
                        pe.wait_ge(o_ready, at(t, 2, 1))
                for h in range(HG):
                    last = pe.matmul(VB[HD * h:HD * h + HD, :], vals[:, j, P * g + HD * h:P * g + HD * h + HD],
                                     pT[:, h, j, :], start=(j == 0), stop=(j == NT - 1), tile_position=(0, HD * h))
                last.then_inc(av_ps, 1)

            def turn_inverse(t, g):
                pe.wait_ge(invx_ready, at(t, 2, g + 1))
                k = turn_of_inv[g]
                wait_bank(t, k)
                for n in range(NT):
                    last = pe.transpose(TB[k % 2][:, tile(n)], inv_x[:, n, :, :].rearrange("p h d -> p (h d)"), ident[:, :])
                last.then_inc(b_turned, 1)

            def project_o(t):
                pe.wait_ge(o_ready, at(t, 2, 2))
                for n in range(NT):
                    if n >= 2:
                        pe.wait_ge(x2_ready, at(t, 4, n - 1))
                    for g in range(DT):
                        last = pe.matmul(SB_[n % 2][:, 0:D], bT[:, g, tile(n)], ws[:, WO, g, :], start=(g == 0), stop=(g == DT - 1))
                    last.then_inc(o_ps, 1)

            def support(t):
                pe.wait_ge(bT_act, at(t, 2, 2))
                for n in range(2):
                    pe.matmul(SB_[n][:, 0:D], bT[:, 0, tile(n)], ws[:, WG, 0, :], start=True, stop=False)
                pe.wait_ge(bT_dve, at(t, 2, 2))
                for n in range(2):
                    pe.matmul(SB_[n][:, 0:D], bT[:, 1, tile(n)], ws[:, WG, 1, :], start=False, stop=True).then_inc(sup_ps, 1)
                for n in range(2, NT):
                    pe.wait_ge(sup_ready, at(t, 4, n - 1))
                    for k in range(DT):
                        last = pe.matmul(SB_[n % 2][:, 0:D], bT[:, k, tile(n)], ws[:, WG, k, :], start=(k == 0), stop=(k == DT - 1))
                    last.then_inc(sup_ps, 1)

            def aggregate3(t):
                pe.wait_ge(adjT_b_loaded, at(t, 16, 16))
                pe.wait_ge(sup_ready, at(t, 4, 4))
                for n in range(NT):
                    if n >= 2:
                        pe.wait_ge(out_ready, at(t, 4, n - 1))
                    for m in range(NT):
                        last = pe.matmul(SB_[n % 2][:, 0:D], adjT_b[:, m, tile(n)], vals[:, m, :], start=(m == 0), stop=(m == NT - 1))
                    last.then_inc(agg3_ps, 1)

            def phases(t, tf):
                b, f = t is not None, tf is not None
                if b:
                    turn(t, 0, 0)
                    project_qk(t, 0, 0)
                    project_qk(t, 0, 1)
                    project_v(t, 0)
                if f:
                    aggregate(tf)
                if b:
                    project_v(t, 1)
                for g in GRID:
                    if b and 0 <= g < 4 * H - 4:
                        scores(t, g + 4)
                    if b and 4 * HG <= g < 4 * HG + 4:
                        attend(t, 0, g - 4 * HG)
                    if f:
                        for n, u in tile_steps(g):
                            if u in (0, 1):
                                hidden(tf, n, u)
                            elif u in (5, 6):
                                turn_hidden(tf, n, u - 5)
                            for q in quarters(n, u):
                                down(tf, n, q)
                    if b and g < 0:
                        scores(t, g + 4)
                    if b and g == Q1_STEP:
                        project_qk(t, 1, 0)
                    if b and g == K1_STEP:
                        project_qk(t, 1, 1)
                    if b and g >= 0:
                        turn_probs(t, g // 4, g % 4)
                    if b and g == 4 * HG + 3:
                        turn_inverse(t, 0)
                if b:
                    turn_inverse(t, 1)
                    for j in range(NT):
                        attend(t, 1, j)
                if f:
                    turn1(tf)
                if b:
                    project_o(t)
                if f:
                    linear(tf)
                if b:
                    turn(t, 1, turn_of_L3)
                    support(t)
                if f:
                    attend1(tf)
                if b:
                    aggregate3(t)

            phases(None, 0)
            phases(0, 1)
            with pe.Fori(1, B - 1) as t:
                phases(t, t + 1)
            phases(B - 1, None)


def kernel(x, adj, nodemask, L0_gnn_epsilon, L0_gnn_W1, L0_gnn_b1, L0_gnn_rms_weight, L0_gnn_W2, L0_gnn_b2,
           L1_gnn_W, L1_gnn_b, L1_gnn_a1, L1_gnn_a2, L1_gnn_att_b, L2_gnn_W_q, L2_gnn_W_k, L2_gnn_W_v, L2_gnn_W_e,
           L2_gnn_W_o, L3_gnn_weight, L3_gnn_bias):
    import numpy as np
    import concourse.bacc as bacc
    from concourse.bass_utils import run_bass_kernel_spmd

    x, adj = np.asarray(x), np.asarray(adj)
    B, N, D = x.shape

    def rows(v, n):
        return np.asarray(v).reshape(n, P).T

    def wide(v, n):
        return np.broadcast_to(np.asarray(v).reshape(1, n), (P, n))

    a = np.stack([rows(L1_gnn_a2, 2), rows(L1_gnn_a1, 2)], axis=-1).reshape(P, 4)
    edge = np.asarray(L2_gnn_W_e).reshape(-1)
    cols = np.concatenate([a, rows(L1_gnn_b, 2), rows(np.repeat(edge, D // edge.size), 2), wide(edge, edge.size),
                           wide(L0_gnn_epsilon, 1), wide(L1_gnn_att_b, 1)], axis=1)
    arrays = {
        "x": x, "adj": adj, "adjT": adj.transpose(0, 2, 1),
        "maskT": np.asarray(nodemask).reshape(B, N // P, P).transpose(0, 2, 1),
        "W1": L0_gnn_W1, "b1": L0_gnn_b1, "rmsw": L0_gnn_rms_weight, "W2": L0_gnn_W2, "b2": L0_gnn_b2,
        "WL": np.asarray(L1_gnn_W).T, "WLn": L1_gnn_W, "bL": L1_gnn_b,
        "WqT": np.asarray(L2_gnn_W_q).T, "WkT": np.asarray(L2_gnn_W_k).T, "WvT": np.asarray(L2_gnn_W_v).T,
        "WoT": np.asarray(L2_gnn_W_o).T, "W3": L3_gnn_weight, "b3": L3_gnn_bias, "cols": cols,
    }
    nc = bacc.Bacc("TRN2", target_bir_lowering=False, num_devices=1)
    ins, args = {}, []
    for name, v in arrays.items():
        v = np.ascontiguousarray(v)
        ins[f"in_{name}"] = v
        args.append(nc.dram_tensor(f"in_{name}", v.shape, mybir.dt.from_np(v.dtype), kind="ExternalInput").ap())
    out = nc.dram_tensor("out", (B, N, D), F32, kind="ExternalOutput").ap()
    gnn_kernel(nc, *args, out)
    r = run_bass_kernel_spmd(nc, [ins], core_ids=[0])
    return r.results[0]["out"]
```
